# Optimizing a Trainium2 kernel written in Bass

```python
import numpy as np
import jax
import jax.numpy as jnp

def _softmax(x, axis=-1):
    return jax.nn.softmax(x, axis=axis)

def _gelu(x):
    return jax.nn.gelu(x, approximate=True)

def _silu(x):
    return jax.nn.silu(x)

def _sigmoid(x):
    return jax.nn.sigmoid(x)

def _layernorm(x, axis=-1, eps=1e-05):
    m = jnp.mean(x, axis=axis, keepdims=True)
    v = jnp.var(x, axis=axis, keepdims=True)
    return (x - m) / jnp.sqrt(v + eps)

def _scatter_add(tgt, idx, src, axis=0):
    return tgt.at[idx].add(src)

def _segment_sum(src, seg, n):
    return jax.ops.segment_sum(src, seg, n)
kernel_name = 'mk_adj_resnorm_d1_adj_r2_bf5a75'

def setup_inputs(seed: int=0):
    np.random.seed(seed)
    _w = jnp.asarray

    def _rec_inputs():
        import jax
        import jax.numpy as jnp
        _gk = jax.random.key(seed)
        x = -0.0002928 + 1 * jax.random.normal(jax.random.fold_in(_gk, 1), (8, 1024, 128), jnp.float32)
        _a = jax.random.bernoulli(jax.random.fold_in(_gk, 2), 0.0078125, (8, 1024, 1024))
        _a = jnp.logical_or(_a, jnp.swapaxes(_a, -1, -2))
        _a = jnp.logical_or(_a, jnp.eye(1024, dtype=bool))
        adj = _a.astype(jnp.int32)
        return (x, adj)
    x, adj = _rec_inputs()

    def _L0_gnn_setup():
        import jax, jax.numpy as jnp
        import numpy as np
        B, N, D_IN, D_OUT, R = (8, 1024, 128, 128, 4)
        key = jax.random.key(seed)
        k1, k2, k3, k4 = jax.random.split(key, 4)
        x = jax.random.normal(k1, (B, N, D_IN), dtype=jnp.float32)
        adj = jnp.zeros((1,), dtype=jnp.float32)
        relation = jax.random.randint(k2, (B, N, N), 0, R + 1, dtype=jnp.int32)
        weight = jax.random.normal(k3, (R, D_IN, D_OUT), dtype=jnp.float32) * 0.05
        bias = jax.random.normal(k4, (D_OUT,), dtype=jnp.float32) * 0.05
        return {'x': x, 'adj': adj, 'relation': relation, 'weight': weight, 'bias': bias}
    _L0_gnn_all = _L0_gnn_setup()
    _L0_gnn_in = {k: v for k, v in _L0_gnn_all.items() if k in ('adj', 'weight', 'bias')}
    del _L0_gnn_all
    return {'x': x, 'adj': adj, 'L0_gnn_adj': _L0_gnn_in['adj'], 'L0_gnn_weight': _L0_gnn_in['weight'], 'L0_gnn_bias': _L0_gnn_in['bias']}

def reference(x, adj, L0_gnn_adj, L0_gnn_weight, L0_gnn_bias):
    import jax
    import jax.numpy as jnp

    def _L0_gnn_ref(x, adj, relation, weight, bias):
        import jax, jax.numpy as jnp
        import numpy as np
        B, N, D_IN, D_OUT, R = (8, 1024, 128, 128, 4)
        rel_ids = jnp.arange(1, weight.shape[0] + 1, dtype=relation.dtype)
        masks = (relation[None] == rel_ids[:, None, None, None]).astype(x.dtype)
        h = jnp.einsum('rbnm,bmd->rbnd', masks, x)
        y = jnp.einsum('rbnd,rdo->bno', h, weight)
        return y + bias
    x = _layernorm(x + _L0_gnn_ref(x, L0_gnn_adj, adj, L0_gnn_weight, L0_gnn_bias), axis=-1)
    return x

_drawn_inputs = setup_inputs


def setup_inputs(seed=0):
    import zlib

    import numpy as np

    out = dict(_drawn_inputs(seed))
    spreads = {}
    factors = {'L0_gnn_bias': 2.706}
    for name, (base, spread) in spreads.items():
        noise = np.random.default_rng([zlib.crc32(name.encode()), seed]).standard_normal(out[name].shape)
        drawn = base * np.exp(spread * noise) if base else spread * noise
        out[name] = jnp.asarray(drawn.astype(out[name].dtype))
    for name, factor in factors.items():
        out[name] = (out[name] * factor).astype(out[name].dtype)
    return out
```

```python
from contextlib import ExitStack

import concourse.bass as bass
from concourse import mybir

P = 128
FP32 = mybir.dt.float32
BF16 = mybir.dt.bfloat16
FP16 = mybir.dt.float16
INT32 = mybir.dt.int32
ALU = mybir.AluOpType
ACT = mybir.ActivationFunctionType
AX = mybir.AxisListType
EPS = 1e-5
TOP = 14
LEAST = 2.0 ** -100
EXPONENT = 0x7F800000


class Group:

    def __init__(self, batch, place, first, count):
        self.batch, self.place, self.first, self.count = batch, place, first, count
        self.index = batch.first_group + place
        self.bank = place % 2
        self.units = range(first, first + count)
        self.cols = slice(first * P, (first + count) * P)


class Batch:

    def __init__(self, b, side, turn, shape, per_batch):
        self.b, self.side, self.turn = b, side, turn
        self.first_group = per_batch * b
        self.groups = [Group(self, n, f, c) for n, (f, c) in enumerate(shape)]


def adj_resnorm_kernel(nc, x, adj, weight, bias, out):
    B, N, D = x.shape
    R = weight.shape[0]
    J = N // P
    PAIRS = J // 2
    GU = 4
    STEADY = [(f, GU) for f in range(0, J, GU)]
    FINAL = [(0, 4), (4, 2), (6, 1), (7, 1)]
    NG = len(STEADY)
    T_BANKS = 4

    x_d = x.rearrange("b (p j) d -> b p j d", j=J)
    adj_d = adj.rearrange("b (p j) m -> b p j m", j=J)
    out_d = out.rearrange("b (p j) d -> b p j d", j=J)

    ctx = ExitStack()
    with ctx:
        def sb(name, shape, dt):
            return ctx.enter_context(nc.sbuf_tensor(name, shape, dt))

        def pb(name, shape, dt):
            return ctx.enter_context(nc.psum_tensor(name, shape, dt))

        def sem(name):
            return ctx.enter_context(nc.semaphore(name))

        ident = sb("ident", [P, P], BF16)
        ones = sb("ones", [P, 1], FP32)
        eps = sb("eps", [P, 1], FP32)
        bias_sb = sb("bias_sb", [P, D], FP32)
        w_sb = sb("w_sb", [P, R, D], FP32)
        adj_sb = sb("adj_sb", [P, 2, J, N], INT32)
        ids = sb("ids", [P, J, J, P], BF16)
        mask_t = sb("mask_t", [P, J, N], BF16)
        x_sb = sb("x_sb", [P, 2, J, D], FP32)
        x_hi = sb("x_hi", [P, 2, J, D], FP16)
        x_lo = sb("x_lo", [P, 2, J, D], FP16)
        xb = sb("xb", [P, 2, J, D], FP32)
        row_max = sb("row_max", [P, 2], FP32)
        clamped = sb("clamped", [P, 2], FP32)
        power = sb("power", [P, 2], FP32)
        down = sb("down", [P, 2], FP32)
        up = sb("up", [P, 2], FP32)
        h_sb = sb("h_sb", [P, N], FP32)
        rows = sb("rows", [P, J, D], FP32)
        stats = sb("stats", [P, J, 6], FP32)
        gap = sb("gap", [P, J], FP32)
        within = sb("within", [P, J], FP32)
        mean2 = sb("mean2", [P, J], FP32)
        spread = sb("spread", [P, J], FP32)
        std = sb("std", [P, J], FP32)
        guess = sb("guess", [P, J], FP32)
        square = sb("square", [P, J], FP32)
        half = sb("half", [P, J], FP32)
        rstd = sb("rstd", [P, J], FP32)
        shift = sb("shift", [P, J], FP32)
        peak = sb("peak", [P, 2, J], FP32)
        excess = sb("excess", [P, J], FP32)
        worst = sb("worst", [P, 1], FP32)
        found = sb("found", [P, 1], FP32)
        again = sb("again", [1, 1], INT32)

        ids_t = [pb(f"ids_t{n}", [P, J, P], BF16) for n in range(T_BANKS)]
        h_ps = [pb(f"h_ps{n}", [P, GU * P], FP32) for n in range(2)]
        y_ps = [pb(f"y_ps{n}", [P, GU, D], FP32) for n in range(2)]

        s_w = sem("weights_loaded")
        s_bias = sem("bias_loaded")
        s_x = [sem(f"x_loaded{n}") for n in range(2)]
        s_adj = [[sem(f"adj_loaded{side}{n}") for n in range(PAIRS)] for side in range(2)]
        s_out = [sem(f"rows_stored{n}") for n in range(len(FINAL))]
        s_zero = sem("ident_zeroed")
        s_ident = sem("ident_ready")
        s_const = sem("constants_ready")
        s_cast = sem("units_cast")
        s_tr = sem("units_transposed")
        s_mask = sem("units_masked")
        s_scale = sem("batches_scaled")
        s_hi = sem("hi_ready")
        s_lo = sem("lo_ready")
        s_xb = sem("xb_ready")
        s_prod = sem("groups_multiplied")
        s_h = sem("h_copied")
        s_y = sem("groups_projected")
        s_sum = sem("groups_summed")
        s_var = sem("variances_ready")
        s_std = sem("std_ready")
        s_rstd = sem("rstd_ready")
        s_half = sem("rows_scaled")
        s_norm = sem("groups_normalised")
        s_found = sem("found_ready")
        s_count = sem("count_ready")
        s_again = sem("again_ready")

        def walk(eng, step, written_out=1):
            def one(cur, nxt, prev):
                for n, g in enumerate(cur.groups):
                    after = cur.groups[n + 1] if n + 1 < len(cur.groups) else (nxt.groups[0] if nxt else None)
                    before = cur.groups[n - 1] if n else (prev.groups[-1] if prev else None)
                    step(g, after, before, nxt)

            def fixed(b):
                return Batch(b, b % 2, b // 2, FINAL if b == B - 1 else STEADY, NG) if 0 <= b < B else None

            one(fixed(0), fixed(1), None)
            with eng.Fori(0, (B - 1 - written_out) // 2) as i:
                one(Batch(2 * i + 1, 1, i, STEADY, NG), Batch(2 * i + 2, 0, i + 1, STEADY, NG),
                    Batch(2 * i, 0, i, STEADY, NG))
                one(Batch(2 * i + 2, 0, i + 1, STEADY, NG), Batch(2 * i + 3, 1, i + 1, STEADY, NG),
                    Batch(2 * i + 1, 1, i, STEADY, NG))
            for b in range(B - written_out, B):
                one(fixed(b), fixed(b + 1), fixed(b - 1))

        def unit_no(g, u):
            return J * g.batch.b + u

        def group_of(g, u):
            return NG * (g.batch.b - 1) + u // GU

        def is_first(batch):
            return isinstance(batch.b, int) and batch.b == 0

        first_pass = ExitStack()
        block = first_pass.enter_context(nc.Block())

        @block.sync
        def _(sp):
            def load_x(batch):
                if not (isinstance(batch.b, int) and batch.b < 2):
                    sp.wait_ge(s_lo, batch.b - 1)
                    sp.wait_ge(s_xb, batch.b - 1)
                sp.dma_start(x_sb[:, batch.side], x_d[batch.b]).then_inc(s_x[batch.side], 16)

            def load_adj(batch, k):
                if not (isinstance(batch.b, int) and batch.b < 2):
                    sp.wait_ge(s_cast, J * (batch.b - 2) + 2 * k + 2)
                sp.dma_start(adj_sb[:, batch.side, 2 * k:2 * k + 2, :],
                             adj_d[batch.b, :, 2 * k:2 * k + 2, :]).then_inc(s_adj[batch.side][k], 16)

            def step(g, after, before, nxt):
                b = g.batch.b
                if not (isinstance(b, int) and b + 2 >= B):
                    coming = Batch(b + 2, g.batch.side, g.batch.turn + 1, STEADY, NG)
                    if g.place == 0:
                        load_x(coming)
                    for k in range(PAIRS // NG * g.place, PAIRS // NG * (g.place + 1)):
                        load_adj(coming, k)
                sp.wait_ge(s_norm, g.index + 1)
                sp.dma_start(out_d[g.batch.b, :, g.first:g.first + g.count, :],
                             rows[:, g.first:g.first + g.count, :]).then_inc(s_out[g.place], 16)

            start = Batch(0, 0, 0, STEADY, NG)
            load_x(start)
            load_adj(start, 0)
            sp.dma_start(w_sb[:, 0, :], weight[0]).then_inc(s_w, 16)
            sp.dma_start(bias_sb[:, :], bias.rearrange("(a d) -> a d", a=1).to_broadcast([P, D])).then_inc(s_bias, 16)
            for k in range(1, PAIRS):
                load_adj(start, k)
            load_x(Batch(1, 1, 0, STEADY, NG))
            for k in range(PAIRS):
                load_adj(Batch(1, 1, 0, STEADY, NG), k)
            walk(sp, step, written_out=3)
            for n in range(len(FINAL)):
                sp.wait_ge(s_out[n], 16 * (B if n < NG else 1))

        @block.gpsimd
        def _(pool):
            nc.gpsimd.memset(ident[:, :], 0.0).then_inc(s_zero, 1)
            pool.wait_ge(s_zero, 1)
            nc.gpsimd.affine_select(out=ident[:, :], in_=ident[:, :], compare_op=ALU.not_equal, fill=1.0,
                                    base=0, pattern=[[-1, P]], channel_multiplier=1).then_inc(s_ident, 1)

            def add_bias(batch):
                pool.wait_ge(s_x[batch.side], 16 * (batch.turn + 1))
                if not (isinstance(batch.b, int) and batch.b < 2):
                    pool.wait_ge(s_sum, NG * (batch.b - 1))
                nc.gpsimd.tensor_tensor(xb[:, batch.side], x_sb[:, batch.side],
                                        bias_sb[:, :].unsqueeze(1).to_broadcast([P, J, D]),
                                        ALU.add).then_inc(s_xb, 1)

            def step(g, after, before, nxt):
                if g.place == 0 and nxt is not None:
                    add_bias(nxt)
                pool.wait_ge(s_rstd, g.index + 1)
                part = rows[:, g.first:g.first + g.count, :]
                wide = [P, g.count, D]
                nc.gpsimd.tensor_tensor(part, part, rstd[:, g.first:g.first + g.count].unsqueeze(2).to_broadcast(wide),
                                        ALU.mult).then_inc(s_half, 1)
                pool.wait_ge(s_half, g.index + 1)
                nc.gpsimd.tensor_tensor(part, part, shift[:, g.first:g.first + g.count].unsqueeze(2).to_broadcast(wide),
                                        ALU.add).then_inc(s_norm, 1)

            pool.wait_ge(s_bias, 16)
            add_bias(Batch(0, 0, 0, STEADY, NG))
            walk(pool, step)

        @block.scalar
        def _(act):
            def cast(g, u):
                act.wait_ge(s_adj[g.batch.side][u // 2], 16 * (g.batch.turn + 1))
                if not is_first(g.batch):
                    act.wait_ge(s_tr, unit_no(g, u) - J + 1)
                nc.scalar.activation(ids[:, u], adj_sb[:, g.batch.side, u, :].rearrange("p (q j) -> p j q", j=J),
                                     ACT.Relu).then_inc(s_cast, 1)

            def split_hi(batch):
                act.wait_ge(s_scale, batch.b + 1)
                if not (isinstance(batch.b, int) and batch.b < 2):
                    act.wait_ge(s_prod, NG * (batch.b - 1))
                nc.scalar.activation(x_hi[:, batch.side], x_sb[:, batch.side], ACT.Copy,
                                     scale=up[:, batch.side:batch.side + 1]).then_inc(s_hi, 1)

            def copy_h(g):
                act.wait_ge(s_prod, g.index + 1)
                if not is_first(g.batch):
                    act.wait_ge(s_y, group_of(g, g.units[-1]) + 1)
                nc.scalar.activation(h_sb[:, g.cols], h_ps[g.bank][:, 0:g.count * P], ACT.Copy).then_inc(s_h, 1)

            def root(g):
                act.wait_ge(s_var, g.index + 1)
                nc.scalar.activation(std[:, g.first:g.first + g.count], spread[:, g.first:g.first + g.count],
                                     ACT.Sqrt, bias=eps[:, 0:1], scale=1.0 / D).then_inc(s_std, 1)

            def step(g, after, before, nxt):
                units = list(after.units) if after else []
                for n, u in enumerate(units):
                    cast(after, u)
                    if n == 0 and before:
                        copy_h(before)
                    if n == 0 and g.place == NG - 1 and nxt is not None:
                        split_hi(nxt)
                    if n == min(2, len(units) - 1) and before:
                        root(before)
                if not units and before:
                    copy_h(before)
                    root(before)
                if after is None:
                    copy_h(g)
                    root(g)

            act.wait_ge(s_const, 1)
            start = Batch(0, 0, 0, STEADY, NG)
            cast(start.groups[0], 0)
            split_hi(start)
            for u in start.groups[0].units[1:]:
                cast(start.groups[0], u)
            walk(act, step)

        @block.tensor
        def _(pe):
            def transpose_unit(g, u):
                pe.wait_ge(s_cast, unit_no(g, u) + 1)
                bank = ids_t[u % T_BANKS]
                if not (is_first(g.batch) and u < T_BANKS):
                    pe.wait_ge(s_mask, unit_no(g, u) - T_BANKS + 1)
                for j in range(J):
                    last = nc.tensor.transpose(bank[:, j, :], ids[:, u, j, :], ident[:, :])
                last.then_inc(s_tr, 1)

            def products(g, n, of):
                todo = [(j, part) for j in range(J) for part in (x_hi, x_lo)]
                lo, hi = len(todo) * n // of, len(todo) * (n + 1) // of
                if n == 0:
                    pe.wait_ge(s_mask, unit_no(g, g.units[-1]) + 1)
                    pe.wait_ge(s_hi, g.batch.b + 1)
                    pe.wait_ge(s_lo, g.batch.b + 1)
                    if not (is_first(g.batch) and g.place < 2):
                        pe.wait_ge(s_h, g.index - 1)
                for j, part in todo[lo:hi]:
                    last = nc.tensor.matmul(h_ps[g.bank][:, 0:g.count * P], part[:, g.batch.side, j, :],
                                            mask_t[:, j, g.cols], start=(j == 0 and part is x_hi),
                                            stop=(j == J - 1 and part is x_lo))
                if hi == len(todo):
                    last.then_inc(s_prod, 1)

            def project(g):
                pe.wait_ge(s_h, g.index + 1)
                if not (is_first(g.batch) and g.place < 2):
                    pe.wait_ge(s_sum, g.index - 1)
                for n, u in enumerate(g.units):
                    last = nc.tensor.matmul(y_ps[g.bank][:, n, :], h_sb[:, u * P:(u + 1) * P], w_sb[:, 0, :],
                                            start=True, stop=True)
                last.then_inc(s_y, 1)

            def step(g, after, before, nxt):
                units = list(after.units) if after else []
                of = max(2, len(units))
                for n in range(of):
                    products(g, n, of)
                    if n == 1 and before:
                        project(before)
                    if n < len(units):
                        transpose_unit(after, units[n])
                if after is None:
                    pe.wait_ge(s_found, 1)
                    nc.tensor.matmul(ids_t[0][0:1, 0, 0:2].bitcast(FP32), found[:, :], ones[:, :],
                                     start=True, stop=True).then_inc(s_count, 1)
                    project(g)

            pe.wait_ge(s_ident, 1)
            start = Batch(0, 0, 0, STEADY, NG)
            for u in start.groups[0].units:
                transpose_unit(start.groups[0], u)
            pe.wait_ge(s_w, 16)
            walk(pe, step)

        @block.vector
        def _(dve):
            def scale(batch):
                dve.wait_ge(s_x[batch.side], 16 * (batch.turn + 1))
                s = slice(batch.side, batch.side + 1)
                rm = nc.vector.tensor_reduce(row_max[:, s], x_sb[:, batch.side], AX.XY, ALU.max,
                                             apply_absolute_value=True)
                rm.then_inc(s_rm, 1)
                dve.wait_ge(s_rm, batch.b + 1)
                nc.vector.tensor_scalar(clamped[:, s], row_max[:, s], LEAST, None, ALU.max).then_inc(s_cl, 1)
                dve.wait_ge(s_cl, batch.b + 1)
                nc.vector.tensor_scalar(power[:, s].bitcast(INT32), clamped[:, s].bitcast(INT32), EXPONENT, None,
                                        ALU.bitwise_and).then_inc(s_pw, 1)
                dve.wait_ge(s_pw, batch.b + 1)
                nc.vector.tensor_scalar(down[:, s], power[:, s], 2.0 ** -TOP, None, ALU.mult).then_inc(s_dn, 1)
                dve.wait_ge(s_dn, batch.b + 1)
                nc.vector.reciprocal(up[:, s], down[:, s]).then_inc(s_scale, 1)

            def split_lo(batch):
                dve.wait_ge(s_hi, batch.b + 1)
                if not (isinstance(batch.b, int) and batch.b < 2):
                    dve.wait_ge(s_prod, NG * (batch.b - 1))
                nc.vector.scalar_tensor_tensor(out=x_lo[:, batch.side], in0=x_sb[:, batch.side],
                                               scalar=up[:, batch.side:batch.side + 1], in1=x_hi[:, batch.side],
                                               op0=ALU.mult, op1=ALU.subtract).then_inc(s_lo, 1)

            def mask_unit(g, u):
                dve.wait_ge(s_tr, unit_no(g, u) + 1)
                if not is_first(g.batch):
                    dve.wait_ge(s_prod, group_of(g, u) + 1)
                side = g.batch.side
                nc.vector.tensor_scalar(mask_t[:, :, u * P:(u + 1) * P], ids_t[u % T_BANKS][:, :, :],
                                        down[:, side:side + 1], None, ALU.mult, ALU.max,
                                        accum_out=peak[:, side, u:u + 1]).then_inc(s_mask, 1)

            def compare(batch):
                dve.wait_ge(s_mask, J * (batch.b + 1))
                if not is_first(batch):
                    dve.wait_ge(s_cmp, batch.b)
                else:
                    dve.wait_ge(s_cmp0, 1)
                nc.vector.scalar_tensor_tensor(out=excess[:, :], in0=peak[:, batch.side], scalar=down[:, batch.side:batch.side + 1],
                                               in1=excess[:, :], op0=ALU.subtract, op1=ALU.max).then_inc(s_cmp, 1)

            def sum_rows(g):
                dve.wait_ge(s_y, g.index + 1)
                dve.wait_ge(s_xb, g.batch.b + 1)
                if not is_first(g.batch):
                    for n in sorted({u // GU for u in g.units}):
                        dve.wait_ge(s_out[n], 16 * g.batch.b)
                us = slice(g.first, g.first + g.count)
                nc.vector.tensor_tensor(rows[:, us, :], y_ps[g.bank][:, 0:g.count, :], xb[:, g.batch.side, us, :],
                                        ALU.add).then_inc(s_sum, 1)
                dve.wait_ge(s_sum, g.index + 1)
                for u in g.units:
                    last = nc.vector.bn_stats(stats[:, u, :], rows[:, u, :])
                last.then_inc(s_st, 1)
                dve.wait_ge(s_st, g.index + 1)
                even, odd = stats[:, us, 0:3], stats[:, us, 3:6]
                nc.vector.tensor_tensor(gap[:, us], even[:, :, 1], odd[:, :, 1], ALU.subtract).then_inc(s_gap, 1)
                nc.vector.tensor_tensor(mean2[:, us], even[:, :, 1], odd[:, :, 1], ALU.add)
                nc.vector.tensor_tensor(within[:, us], even[:, :, 2], odd[:, :, 2], ALU.add).then_inc(s_within, 1)
                dve.wait_ge(s_gap, g.index + 1)
                nc.vector.tensor_tensor(gap[:, us], gap[:, us], gap[:, us], ALU.mult).then_inc(s_gap2, 1)
                dve.wait_ge(s_gap2, g.index + 1)
                dve.wait_ge(s_within, g.index + 1)
                nc.vector.scalar_tensor_tensor(out=spread[:, us], in0=gap[:, us], scalar=D / 4.0, in1=within[:, us],
                                               op0=ALU.mult, op1=ALU.add).then_inc(s_var, 1)

            def invert_root(g):
                dve.wait_ge(s_std, g.index + 1)
                us = slice(g.first, g.first + g.count)
                nc.vector.reciprocal(guess[:, us], std[:, us]).then_inc(s_n[0], 1)
                dve.wait_ge(s_n[0], g.index + 1)
                nc.vector.tensor_tensor(square[:, us], guess[:, us], guess[:, us], ALU.mult).then_inc(s_n[1], 1)
                dve.wait_ge(s_n[1], g.index + 1)
                nc.vector.scalar_tensor_tensor(out=half[:, us], in0=spread[:, us], scalar=D * EPS,
                                               in1=square[:, us], op0=ALU.add, op1=ALU.mult).then_inc(s_n[2], 1)
                dve.wait_ge(s_n[2], g.index + 1)
                nc.vector.tensor_scalar(square[:, us], half[:, us], -0.5 / D, 1.5, ALU.mult, ALU.add).then_inc(s_n[3], 1)
                dve.wait_ge(s_n[3], g.index + 1)
                if not is_first(g.batch):
                    dve.wait_ge(s_norm, group_of(g, g.units[-1]) + 1)
                nc.vector.tensor_tensor(rstd[:, us], guess[:, us], square[:, us], ALU.mult).then_inc(s_n[4], 1)
                dve.wait_ge(s_n[4], g.index + 1)
                nc.vector.scalar_tensor_tensor(out=shift[:, us], in0=mean2[:, us], scalar=-0.5,
                                               in1=rstd[:, us], op0=ALU.mult, op1=ALU.mult).then_inc(s_rstd, 1)

            def step(g, after, before, nxt):
                units = list(after.units) if after else []
                if g.place == NG - 1 and nxt is not None:
                    scale(nxt)
                for n, u in enumerate(units):
                    mask_unit(after, u)
                    if n == min(1, len(units) - 1) and before:
                        sum_rows(before)
                if not units and before:
                    sum_rows(before)
                if before:
                    invert_root(before)
                if g.place == NG - 1 and nxt is not None:
                    split_lo(nxt)
                if after is not None and after.batch is g.batch and after.place == len(g.batch.groups) - 1:
                    compare(g.batch)
                if after is None:
                    nc.vector.tensor_reduce(worst[:, :], excess[:, :], AX.X, ALU.max).then_inc(s_worst, 1)
                    dve.wait_ge(s_worst, 1)
                    nc.vector.tensor_scalar(found[:, :], worst[:, :], 0.0, None, ALU.is_gt).then_inc(s_found, 1)
                    dve.wait_ge(s_count, 1)
                    nc.vector.tensor_copy(again[:, :], ids_t[0][0:1, 0, 0:2].bitcast(FP32)).then_inc(s_again, 1)
                    sum_rows(g)
                    invert_root(g)

            s_rm, s_cl, s_pw, s_dn = (sem(n) for n in ("row_max_ready", "clamped_ready", "power_ready", "down_ready"))
            s_st = sem("stats_ready")
            s_gap, s_gap2, s_within = (sem(n) for n in ("gap_ready", "gap_squared", "within_ready"))
            s_cmp, s_cmp0 = sem("batches_compared"), sem("excess_zeroed")
            s_worst = sem("worst_ready")
            s_n = [sem(f"newton{n}") for n in range(5)]
            nc.vector.memset(eps[:, :], EPS)
            nc.vector.memset(ones[:, :], 1.0)
            nc.vector.memset(excess[:, :], 0.0).then_inc(s_cmp0, 1)
            dve.wait_ge(s_cmp0, 1)
            nc.vector.memset(worst[:, :], 0.0).then_inc(s_const, 1)
            start = Batch(0, 0, 0, STEADY, NG)
            scale(start)
            mask_unit(start.groups[0], 0)
            split_lo(start)
            for u in start.groups[0].units[1:]:
                mask_unit(start.groups[0], u)
            walk(dve, step)

        first_pass.close()

        g_w = sem("g_weights_loaded")
        g_x = sem("g_x_loaded")
        g_adj = [sem(f"g_adj_loaded{n}") for n in range(PAIRS)]
        g_out, g_batch = sem("g_rows_stored"), sem("g_batches_stored")
        g_max, g_clamp, g_power, g_down, g_scale = (sem(f"g_{n}") for n in ("max", "clamp", "power", "down", "scale"))
        g_hi, g_lo, g_xb = sem("g_hi_ready"), sem("g_lo_ready"), sem("g_xb_ready")
        g_cast, g_tr, g_mask = sem("g_units_cast"), sem("g_units_transposed"), sem("g_units_masked")
        g_prod, g_h, g_y = sem("g_products_done"), sem("g_h_copied"), sem("g_projected")
        g_sum, g_stats, g_gap, g_var = sem("g_summed"), sem("g_stats"), sem("g_gap"), sem("g_var")
        g_std, g_norm = sem("g_std"), sem("g_normalised")
        g_newton = [sem(f"g_newton{n}") for n in range(6)]
        g_gap2 = sem("g_gap_squared")

        def halves(t, n):
            return t[..., n * GU * P:(n + 1) * GU * P]

        def second_pass():
            with nc.Block() as block:
                @block.sync
                def _(sp):
                    sp.dma_start(w_sb[:, 1:R, :], weight[1:R].rearrange("r d o -> d r o")).then_inc(g_w, 16)
                    with sp.Fori(0, B) as b:
                        sp.dma_start(x_sb[:, 0], x_d[b]).then_inc(g_x, 16)
                        for k in range(PAIRS):
                            sp.dma_start(adj_sb[:, 0, 2 * k:2 * k + 2, :],
                                         adj_d[b, :, 2 * k:2 * k + 2, :]).then_inc(g_adj[k], 16)
                        for g in range(NG):
                            sp.wait_ge(g_norm, NG * b + g + 1)
                            sp.dma_start(out_d[b, :, g * GU:(g + 1) * GU, :],
                                         rows[:, g * GU:(g + 1) * GU, :]).then_inc(g_out, 16)
                        sp.wait_ge(g_out, 16 * NG * (b + 1))
                        sp.sem_inc(g_batch, 1)

                @block.gpsimd
                def _(pool):
                    with pool.Fori(0, B) as b:
                        pool.wait_ge(g_x, 16 * (b + 1))
                        nc.gpsimd.tensor_tensor(xb[:, 0], x_sb[:, 0],
                                                bias_sb[:, :].unsqueeze(1).to_broadcast([P, J, D]),
                                                ALU.add).then_inc(g_xb, 1)

                @block.scalar
                def _(act):
                    with act.Fori(0, B) as b:
                        for u in range(J):
                            act.wait_ge(g_adj[u // 2], 16 * (b + 1))
                            nc.scalar.activation(ids[:, u], adj_sb[:, 0, u, :].rearrange("p (q j) -> p j q", j=J),
                                                 ACT.Relu).then_inc(g_cast, 1)
                        act.wait_ge(g_scale, b + 1)
                        nc.scalar.activation(x_hi[:, 0], x_sb[:, 0], ACT.Copy, scale=up[:, 0:1]).then_inc(g_hi, 1)
                        for g in range(NG):
                            for r in range(R):
                                done = R * (NG * b + g) + r
                                act.wait_ge(g_prod, done + 1)
                                if r >= 2:
                                    act.wait_ge(g_y, done - 1)
                                nc.scalar.activation(halves(h_sb, r % 2), h_ps[r % 2][:, :], ACT.Copy).then_inc(g_h, 1)
                            act.wait_ge(g_var, NG * b + g + 1)
                            us = slice(g * GU, (g + 1) * GU)
                            nc.scalar.activation(std[:, us], spread[:, us], ACT.Sqrt, bias=eps[:, 0:1],
                                                 scale=1.0 / D).then_inc(g_std, 1)

                @block.tensor
                def _(pe):
                    pe.wait_ge(g_w, 16)
                    with pe.Fori(0, B) as b:
                        for g in range(NG):
                            for n in range(GU):
                                pe.wait_ge(g_cast, J * b + GU * g + n + 1)
                                if g:
                                    pe.wait_ge(g_mask, R * GU * (NG * b + g))
                                for j in range(J):
                                    last = nc.tensor.transpose(ids_t[n][:, j, :], ids[:, g * GU + n, j, :], ident[:, :])
                                last.then_inc(g_tr, 1)
                            pe.wait_ge(g_hi, b + 1)
                            pe.wait_ge(g_lo, b + 1)
                            for r in range(R + 1):
                                done = R * (NG * b + g) + r
                                if r < R:
                                    pe.wait_ge(g_mask, GU * (done + 1))
                                    if r >= 2:
                                        pe.wait_ge(g_h, done - 1)
                                    for j in range(J):
                                        for part in (x_hi, x_lo):
                                            last = nc.tensor.matmul(
                                                h_ps[r % 2][:, :], part[:, 0, j, :], halves(mask_t[:, j, :], r % 2),
                                                start=(j == 0 and part is x_hi), stop=(j == J - 1 and part is x_lo))
                                    last.then_inc(g_prod, 1)
                                if r > 0:
                                    pe.wait_ge(g_h, done)
                                    for n in range(GU):
                                        cols = slice(((r - 1) % 2 * GU + n) * P, ((r - 1) % 2 * GU + n + 1) * P)
                                        last = nc.tensor.matmul(y_ps[0][:, n, :],
                                                                h_sb[:, cols], w_sb[:, r - 1, :],
                                                                start=(r == 1 and n == 0), stop=(r == R))
                                    last.then_inc(g_y, 1)

                @block.vector
                def _(dve):
                    with dve.Fori(0, B) as b:
                        dve.wait_ge(g_x, 16 * (b + 1))
                        nc.vector.tensor_reduce(row_max[:, 0:1], x_sb[:, 0], AX.XY, ALU.max,
                                                apply_absolute_value=True).then_inc(g_max, 1)
                        dve.wait_ge(g_max, b + 1)
                        nc.vector.tensor_scalar(clamped[:, 0:1], row_max[:, 0:1], LEAST, None, ALU.max).then_inc(g_clamp, 1)
                        dve.wait_ge(g_clamp, b + 1)
                        nc.vector.tensor_scalar(power[:, 0:1].bitcast(INT32), clamped[:, 0:1].bitcast(INT32), EXPONENT,
                                                None, ALU.bitwise_and).then_inc(g_power, 1)
                        dve.wait_ge(g_power, b + 1)
                        nc.vector.tensor_scalar(down[:, 0:1], power[:, 0:1], 2.0 ** -TOP, None, ALU.mult).then_inc(g_down, 1)
                        dve.wait_ge(g_down, b + 1)
                        nc.vector.reciprocal(up[:, 0:1], down[:, 0:1]).then_inc(g_scale, 1)
                        dve.wait_ge(g_hi, b + 1)
                        nc.vector.scalar_tensor_tensor(out=x_lo[:, 0], in0=x_sb[:, 0], scalar=up[:, 0:1], in1=x_hi[:, 0],
                                                       op0=ALU.mult, op1=ALU.subtract).then_inc(g_lo, 1)
                        for g in range(NG):
                            us = slice(g * GU, (g + 1) * GU)
                            for r in range(R):
                                if r >= 2:
                                    dve.wait_ge(g_prod, R * (NG * b + g) + r - 1)
                                for n in range(GU):
                                    dve.wait_ge(g_tr, J * b + GU * g + n + 1)
                                    at = (r % 2 * GU + n) * P
                                    nc.vector.tensor_scalar(mask_t[:, :, at:at + P], ids_t[n][:, :, :], float(r + 1),
                                                            down[:, 0:1], ALU.is_equal, ALU.mult).then_inc(g_mask, 1)
                            dve.wait_ge(g_xb, b + 1)
                            dve.wait_ge(g_y, R * (NG * b + g + 1))
                            nc.vector.tensor_tensor(rows[:, us, :], y_ps[0][:, :, :], xb[:, 0, us, :], ALU.add).then_inc(g_sum, 1)
                            dve.wait_ge(g_sum, NG * b + g + 1)
                            for u in range(g * GU, (g + 1) * GU):
                                last = nc.vector.bn_stats(stats[:, u, :], rows[:, u, :])
                            last.then_inc(g_stats, 1)
                            dve.wait_ge(g_stats, NG * b + g + 1)
                            even, odd = stats[:, us, 0:3], stats[:, us, 3:6]
                            nc.vector.tensor_tensor(gap[:, us], even[:, :, 1], odd[:, :, 1], ALU.subtract)
                            nc.vector.tensor_tensor(mean2[:, us], even[:, :, 1], odd[:, :, 1], ALU.add)
                            nc.vector.tensor_tensor(within[:, us], even[:, :, 2], odd[:, :, 2], ALU.add).then_inc(g_gap, 1)
                            dve.wait_ge(g_gap, NG * b + g + 1)
                            nc.vector.tensor_tensor(gap[:, us], gap[:, us], gap[:, us], ALU.mult).then_inc(g_gap2, 1)
                            dve.wait_ge(g_gap2, NG * b + g + 1)
                            nc.vector.scalar_tensor_tensor(out=spread[:, us], in0=gap[:, us], scalar=D / 4.0,
                                                           in1=within[:, us], op0=ALU.mult, op1=ALU.add).then_inc(g_var, 1)
                            dve.wait_ge(g_std, NG * b + g + 1)
                            nc.vector.reciprocal(guess[:, us], std[:, us]).then_inc(g_newton[0], 1)
                            dve.wait_ge(g_newton[0], NG * b + g + 1)
                            nc.vector.tensor_tensor(square[:, us], guess[:, us], guess[:, us], ALU.mult).then_inc(g_newton[1], 1)
                            dve.wait_ge(g_newton[1], NG * b + g + 1)
                            nc.vector.scalar_tensor_tensor(out=half[:, us], in0=spread[:, us], scalar=D * EPS,
                                                           in1=square[:, us], op0=ALU.add, op1=ALU.mult).then_inc(g_newton[2], 1)
                            dve.wait_ge(g_newton[2], NG * b + g + 1)
                            nc.vector.tensor_scalar(square[:, us], half[:, us], -0.5 / D, 1.5, ALU.mult, ALU.add).then_inc(g_newton[3], 1)
                            dve.wait_ge(g_newton[3], NG * b + g + 1)
                            nc.vector.tensor_tensor(rstd[:, us], guess[:, us], square[:, us], ALU.mult).then_inc(g_newton[4], 1)
                            dve.wait_ge(g_newton[4], NG * b + g + 1)
                            nc.vector.scalar_tensor_tensor(out=shift[:, us], in0=mean2[:, us], scalar=-0.5,
                                                           in1=rstd[:, us], op0=ALU.mult, op1=ALU.mult).then_inc(g_newton[5], 1)
                            dve.wait_ge(g_newton[5], NG * b + g + 1)
                            for u in range(g * GU, (g + 1) * GU):
                                last = nc.vector.tensor_scalar(rows[:, u, :], rows[:, u, :], rstd[:, u:u + 1],
                                                               shift[:, u:u + 1], ALU.mult, ALU.add)
                            last.then_inc(g_norm, 1)

        high = nc.values_load(again[0:1, 0:1], min_val=0, max_val=P)
        with nc.If(high > 0):
            second_pass()


def kernel(x, adj, L0_gnn_adj, L0_gnn_weight, L0_gnn_bias):
    import numpy as np
    import concourse.bacc as bacc
    from concourse.bass_utils import run_bass_kernel_spmd

    nc = bacc.Bacc("TRN2", target_bir_lowering=False, num_devices=1)
    arrays = {"x": np.ascontiguousarray(x), "adj": np.ascontiguousarray(adj),
              "weight": np.ascontiguousarray(L0_gnn_weight), "bias": np.ascontiguousarray(L0_gnn_bias)}
    args = [nc.dram_tensor(name, a.shape, mybir.dt.from_np(a.dtype), kind="ExternalInput").ap()
            for name, a in arrays.items()]
    out = nc.dram_tensor("out", arrays["x"].shape, FP32, kind="ExternalOutput").ap()
    adj_resnorm_kernel(nc, *args, out)
    return run_bass_kernel_spmd(nc, [arrays], core_ids=[0]).results[0]["out"]
```

```python
from contextlib import ExitStack

import concourse.bass as bass
from concourse import mybir

P = 128
FP32 = mybir.dt.float32
BF16 = mybir.dt.bfloat16
FP16 = mybir.dt.float16
INT32 = mybir.dt.int32
ALU = mybir.AluOpType
ACT = mybir.ActivationFunctionType
AX = mybir.AxisListType
EPS = 1e-5
TOP = 14
SPAN = 2.0 ** 14
LEAST = 2.0 ** -100
EXPONENT = 0x7F800000


class Group:

    def __init__(self, batch, place, first, count):
        self.batch, self.place, self.first, self.count = batch, place, first, count
        self.index = batch.first_group + place
        self.bank = place % 2
        self.units = range(first, first + count)
        self.cols = slice(first * P, (first + count) * P)


class Batch:

    def __init__(self, b, side, turn, shape, per_batch):
        self.b, self.side, self.turn = b, side, turn
        self.first_group = per_batch * b
        self.groups = [Group(self, n, f, c) for n, (f, c) in enumerate(shape)]


def adj_resnorm_kernel(nc, x, adj, weight, bias, out):
    B, N, D = x.shape
    R = weight.shape[0]
    J = N // P
    PAIRS = J // 2
    GU = 4
    STEADY = [(f, GU) for f in range(0, J, GU)]
    FINAL = [(0, 4), (4, 3), (7, 1)]
    NG = len(STEADY)
    T_BANKS = 4
    AHEAD = 2
    STP = 0
    DL = 4
    PROJ = 1

    x_d = x.rearrange("b (p j) d -> b p j d", j=J)
    adj_d = adj.rearrange("b (p j) m -> b p j m", j=J)
    out_d = out.rearrange("b (p j) d -> b p j d", j=J)

    ctx = ExitStack()
    with ctx:
        def sb(name, shape, dt):
            return ctx.enter_context(nc.sbuf_tensor(name, shape, dt))

        def pb(name, shape, dt):
            return ctx.enter_context(nc.psum_tensor(name, shape, dt))

        def sem(name):
            return ctx.enter_context(nc.semaphore(name))

        ident = sb("ident", [P, P], BF16)
        ones = sb("ones", [P, 1], FP32)
        eps = sb("eps", [P, 1], FP32)
        bias_sb = sb("bias_sb", [P, D], FP32)
        w_sb = sb("w_sb", [P, R, D], FP32)
        adj_sb = sb("adj_sb", [P, 2, J, N], INT32)
        ids = sb("ids", [P, J, J, P], BF16)
        mask_t = sb("mask_t", [P, J, N], BF16)
        x_sb = sb("x_sb", [P, 2, J, D], FP32)
        x_up = sb("x_up", [P, J, D], FP32)
        x_hi = sb("x_hi", [P, 2, J, D], FP16)
        x_lo = sb("x_lo", [P, 2, J, D], FP16)
        xb = sb("xb", [P, 2, J, D], FP32)
        row_max = sb("row_max", [P, J], FP32)
        largest = sb("largest", [P, 1], FP32)
        power = sb("power", [P, 1], FP32)
        down = sb("down", [P, 2], FP32)
        up = sb("up", [P, 2], FP32)
        h_all = sb("h_all", [P, R, GU * P], FP32)
        h_sb = h_all[:, 0:N // (GU * P), :].rearrange("p r n -> p (r n)")
        rows = sb("rows", [P, 2, J, D], FP32)
        stats = sb("stats", [P, J, 6], FP32)
        gap = sb("gap", [P, J], FP32)
        within = sb("within", [P, J], FP32)
        mean2 = sb("mean2", [P, J], FP32)
        spread = sb("spread", [P, J], FP32)
        std = sb("std", [P, J], FP32)
        guess = sb("guess", [P, J], FP32)
        square = sb("square", [P, J], FP32)
        half = sb("half", [P, J], FP32)
        rstd = sb("rstd", [P, J], FP32)
        shift = sb("shift", [P, J], FP32)
        far = sb("far", [P, J], FP32)
        unsuited = sb("unsuited", [P, J], FP32)
        peak = sb("peak", [P, 2, J], FP32)
        excess = sb("excess", [P, J], FP32)
        worst = sb("worst", [P, 1], FP32)
        found = sb("found", [P, 1], FP32)
        again = sb("again", [1, 1], INT32)

        ids_t = [pb(f"ids_t{n}", [P, J, P], BF16) for n in range(T_BANKS)]
        h_ps = [pb(f"h_ps{n}", [P, GU * P], FP32) for n in range(2)]
        y_ps = [pb(f"y_ps{n}", [P, GU, D], FP32) for n in range(2)]

        s_w = sem("weights_loaded")
        s_bias = sem("bias_loaded")
        s_x = [sem(f"x_loaded{n}") for n in range(2)]
        s_adj = [[sem(f"adj_loaded{side}{n}") for n in range(PAIRS)] for side in range(2)]
        s_out = [[sem(f"rows_stored{side}{n}") for n in range(len(FINAL))] for side in range(2)]
        s_zero = sem("ident_zeroed")
        s_ident = sem("ident_ready")
        s_const = sem("constants_ready")
        s_cast = sem("units_cast")
        s_tr = sem("units_transposed")
        s_mask = sem("units_masked")
        s_scale = sem("batches_scaled")
        s_up = sem("x_scaled")
        s_hi = sem("hi_ready")
        s_lo = sem("lo_ready")
        s_xb = sem("xb_ready")
        s_prod = sem("groups_multiplied")
        s_h = sem("h_copied")
        s_y = sem("groups_projected")
        s_sum = sem("groups_summed")
        s_var = sem("variances_ready")
        s_std = sem("std_ready")
        s_rstd = sem("rstd_ready")
        s_half = sem("rows_scaled")
        s_norm = sem("groups_normalised")
        s_found = sem("found_ready")
        s_count = sem("count_ready")
        s_again = sem("again_ready")

        def walk(eng, step, ahead=1, behind=1):
            def one(cur, nxt, prev):
                past = [None, None] if prev is None else prev.groups[-2:]
                order = past + cur.groups + (nxt.groups if nxt else []) + [None, None]
                for n, g in enumerate(cur.groups):
                    step(g, order[n + 3:n + 5], order[n + 1], order[n], nxt)

            def fixed(b):
                return Batch(b, b % 2, b // 2, FINAL if b == B - 1 else STEADY, NG) if 0 <= b < B else None

            def turning(i, n):
                n += ahead
                return Batch(2 * i + n, n % 2, i + n // 2, STEADY, NG)

            for b in range(ahead):
                one(fixed(b), fixed(b + 1), fixed(b - 1))
            with eng.Fori(0, (B - ahead - behind) // 2) as i:
                for n in range(2):
                    one(turning(i, n), turning(i, n + 1), turning(i, n - 1))
            for b in range(B - behind, B):
                one(fixed(b), fixed(b + 1), fixed(b - 1))

        def three_before(g):
            batch = g.batch
            if g.place >= 3:
                return batch.groups[g.place - 3]
            if isinstance(batch.b, int) and NG * batch.b + g.place < 3:
                return None
            if g.place > 0:
                return Batch(batch.b - 1, 1 - batch.side, batch.turn - 1 + batch.side, STEADY, NG).groups[g.place - 1]
            return Batch(batch.b - 2, batch.side, batch.turn - 1, STEADY, NG).groups[1]

            def fixed(b):
                return Batch(b, b % 2, b // 2, FINAL if b == B - 1 else STEADY, NG) if 0 <= b < B else None

            one(fixed(0), Batch(1, 1, 0, STEADY, NG), None)
            with eng.Fori(0, (B - 1 - written_out) // 2) as i:
                one(Batch(2 * i + 1, 1, i, STEADY, NG), Batch(2 * i + 2, 0, i + 1, STEADY, NG),
                    Batch(2 * i, 0, i, STEADY, NG))
                one(Batch(2 * i + 2, 0, i + 1, STEADY, NG), Batch(2 * i + 3, 1, i + 1, STEADY, NG),
                    Batch(2 * i + 1, 1, i, STEADY, NG))
            for b in range(B - written_out, B):
                one(fixed(b), fixed(b + 1), fixed(b - 1))

        def unit_no(g, u):
            return J * g.batch.b + u

        def group_of(g, u):
            return NG * (g.batch.b - 1) + u // GU

        def is_first(batch):
            return isinstance(batch.b, int) and batch.b == 0

        first_pass = ExitStack()
        block = first_pass.enter_context(nc.Block())

        @block.sync
        def _(sp):
            def load_x(batch):
                if not (isinstance(batch.b, int) and batch.b < 2):
                    sp.wait_ge(s_up, batch.b - 1)
                    sp.wait_ge(s_xb, batch.b - 1)
                sp.dma_start(x_sb[:, batch.side], x_d[batch.b]).then_inc(s_x[batch.side], 16)

            def load_adj(batch, k):
                if not (isinstance(batch.b, int) and batch.b < 2):
                    sp.wait_ge(s_cast, J * (batch.b - 2) + 2 * k + 2 + DL)
                sp.dma_start(adj_sb[:, batch.side, 2 * k:2 * k + 2, :],
                             adj_d[batch.b, :, 2 * k:2 * k + 2, :]).then_inc(s_adj[batch.side][k], 16)

            def step(g, coming, before, earlier, nxt):
                b, side, turn = g.batch.b, g.batch.side, g.batch.turn
                if not (isinstance(b, int) and b + 2 >= B):
                    if g.place == NG - 1 and not (isinstance(b, int) and b + 3 >= B):
                        load_x(Batch(b + 3, 1 - side, turn + 1 + side, STEADY, NG))
                    for k in range(PAIRS // NG * g.place, PAIRS // NG * (g.place + 1)):
                        load_adj(Batch(b + 2, side, turn + 1, STEADY, NG), k)

            for side in range(2):
                for n in range(NG):
                    sp.sem_inc(s_out[side][n], 1)
            first, second = (Batch(n, n, 0, STEADY, NG) for n in range(2))
            load_x(first)
            load_adj(first, 0)
            sp.dma_start(w_sb[:, 0, :], weight[0]).then_inc(s_w, 16)
            sp.dma_start(bias_sb[:, :], bias.rearrange("(a d) -> a d", a=1).to_broadcast([P, D])).then_inc(s_bias, 16)
            load_adj(first, 1)
            load_x(second)
            load_adj(first, 2)
            load_adj(first, 3)
            load_adj(second, 0)
            load_adj(second, 1)
            load_x(Batch(2, 0, 1, STEADY, NG))
            load_adj(second, 2)
            load_adj(second, 3)
            walk(sp, step, behind=3)
            for side in range(2):
                for n in range(NG):
                    sp.wait_ge(s_out[side][n], 16 * (B // 2) + 1)
            for n in range(NG, len(FINAL)):
                sp.wait_ge(s_out[(B - 1) % 2][n], 16)

        @block.gpsimd
        def _(pool):
            nc.gpsimd.memset(ident[:, :], 0.0).then_inc(s_zero, 1)
            pool.wait_ge(s_zero, 1)
            nc.gpsimd.affine_select(out=ident[:, :], in_=ident[:, :], compare_op=ALU.not_equal, fill=1.0,
                                    base=0, pattern=[[-1, P]], channel_multiplier=1).then_inc(s_ident, 1)

            def add_bias(batch):
                pool.wait_ge(s_x[batch.side], 16 * (batch.turn + 1))
                if not (isinstance(batch.b, int) and batch.b < 2):
                    pool.wait_ge(s_sum, NG * (batch.b - 1) + 1)
                nc.gpsimd.tensor_tensor(xb[:, batch.side], x_sb[:, batch.side],
                                        bias_sb[:, :].unsqueeze(1).to_broadcast([P, J, D]),
                                        ALU.add).then_inc(s_xb, 1)

            def split_lo(batch):
                pool.wait_ge(s_hi, batch.b + 1)
                if not (isinstance(batch.b, int) and batch.b < 2):
                    pool.wait_ge(s_prod, NG * (batch.b - 1))
                nc.gpsimd.tensor_tensor(x_lo[:, batch.side], x_up[:, :], x_hi[:, batch.side],
                                        ALU.subtract).then_inc(s_lo, 1)

            def normalise(g):
                pool.wait_ge(s_rstd, g.index + 1)
                part = rows[:, g.batch.side, g.first:g.first + g.count, :]
                wide = [P, g.count, D]
                nc.gpsimd.tensor_tensor(part, part, rstd[:, g.first:g.first + g.count].unsqueeze(2).to_broadcast(wide),
                                        ALU.mult).then_inc(s_half, 1)
                pool.wait_ge(s_half, g.index + 1)
                nc.gpsimd.tensor_tensor(part, part, shift[:, g.first:g.first + g.count].unsqueeze(2).to_broadcast(wide),
                                        ALU.add).then_inc(s_norm, 1)

            def step(g, coming, before, earlier, nxt):
                if earlier:
                    normalise(earlier)
                if g.place == 0 and nxt is not None:
                    split_lo(nxt)
                if g.place == NG - 1 and nxt is not None:
                    add_bias(nxt)
                if coming[0] is None:
                    normalise(before)
                    normalise(g)

            split_lo(Batch(0, 0, 0, STEADY, NG))
            pool.wait_ge(s_bias, 16)
            add_bias(Batch(0, 0, 0, STEADY, NG))
            walk(pool, step)

        @block.scalar
        def _(act):
            def cast(batch, u):
                act.wait_ge(s_adj[batch.side][u // 2], 16 * (batch.turn + 1))
                if not is_first(batch):
                    act.wait_ge(s_tr, J * (batch.b - 1) + u + 1)
                nc.scalar.activation(ids[:, u], adj_sb[:, batch.side, u, :].rearrange("p (q j) -> p j q", j=J),
                                     ACT.Relu).then_inc(s_cast, 1)

            def scale_x(batch):
                act.wait_ge(s_scale, batch.b + 1)
                if not is_first(batch):
                    act.wait_ge(s_lo, batch.b)
                nc.scalar.activation(x_up[:, :], x_sb[:, batch.side], ACT.Copy,
                                     scale=up[:, batch.side:batch.side + 1]).then_inc(s_up, 1)

            def split_hi(batch):
                act.wait_ge(s_up, batch.b + 1)
                if not (isinstance(batch.b, int) and batch.b < 2):
                    act.wait_ge(s_prod, NG * (batch.b - 1))
                nc.scalar.activation(x_hi[:, batch.side], x_up[:, :], ACT.Copy).then_inc(s_hi, 1)

            def copy_h(g):
                act.wait_ge(s_prod, g.index + 1)
                nc.scalar.activation(h_sb[:, g.cols], h_ps[g.bank][:, 0:g.count * P], ACT.Copy).then_inc(s_h, 1)

            def root(g):
                act.wait_ge(s_var, g.index + 1)
                nc.scalar.activation(std[:, g.first:g.first + g.count], spread[:, g.first:g.first + g.count],
                                     ACT.Sqrt, bias=eps[:, 0:1], scale=1.0 / D).then_inc(s_std, 1)

            def store(g):
                act.wait_ge(s_norm, g.index + 1)
                act.dma_start(out_d[g.batch.b, :, g.first:g.first + g.count, :],
                              rows[:, g.batch.side, g.first:g.first + g.count, :]).then_inc(s_out[g.batch.side][g.place], 16)

            def step(g, coming, before, earlier, nxt):
                after = coming[0]
                due = [(after.batch, u + AHEAD) for u in after.units] if after else []
                due = [(batch, u) if u < J else (nxt, u - J) for batch, u in due]
                due = [(batch, u) for batch, u in due if batch is not None]

                def cast_next():
                    if due:
                        cast(*due.pop(0))

                if before:
                    copy_h(before)
                if earlier:
                    root(earlier)
                for n in range(GU):
                    if n == STP and three_before(g):
                        store(three_before(g))
                    cast_next()
                if g.place == 0 and nxt is not None:
                    scale_x(nxt)
                    split_hi(nxt)
                if after is None:
                    root(before)
                    copy_h(g)
                    store(earlier)
                    root(g)
                    store(before)
                    store(g)

            act.preload_act_table(ACT.Sqrt)
            act.wait_ge(s_const, 1)
            start = Batch(0, 0, 0, STEADY, NG)
            cast(start, 0)
            scale_x(start)
            split_hi(start)
            for u in range(1, GU + AHEAD):
                cast(start, u)
            walk(act, step, ahead=2, behind=2)

        @block.tensor
        def _(pe):
            def transpose_unit(g, u):
                pe.wait_ge(s_cast, unit_no(g, u) + 1)
                bank = ids_t[u % T_BANKS]
                if not (is_first(g.batch) and u < T_BANKS):
                    pe.wait_ge(s_mask, unit_no(g, u) - T_BANKS + 1)
                for j in range(J):
                    last = nc.tensor.transpose(bank[:, j, :], ids[:, u, j, :], ident[:, :])
                last.then_inc(s_tr, 1)

            def products(g, n, of):
                todo = [(j, part) for part in (x_hi, x_lo) for j in range(J)]
                lo, hi = len(todo) * n // of, len(todo) * (n + 1) // of
                if n == 0:
                    pe.wait_ge(s_mask, unit_no(g, g.units[-1]) + 1)
                    pe.wait_ge(s_hi, g.batch.b + 1)
                    if not (is_first(g.batch) and g.place < 2):
                        pe.wait_ge(s_h, g.index - 1)
                if lo <= J < hi:
                    pe.wait_ge(s_lo, g.batch.b + 1)
                for j, part in todo[lo:hi]:
                    last = nc.tensor.matmul(h_ps[g.bank][:, 0:g.count * P], part[:, g.batch.side, j, :],
                                            mask_t[:, j, g.cols], start=(j == 0 and part is x_hi),
                                            stop=(j == J - 1 and part is x_lo))
                if hi == len(todo):
                    last.then_inc(s_prod, 1)

            def project(g):
                pe.wait_ge(s_h, g.index + 1)
                if not (is_first(g.batch) and g.place < 1):
                    pe.wait_ge(s_sum, g.index)
                for n, u in enumerate(g.units):
                    last = nc.tensor.matmul(y_ps[g.bank][:, n, :], h_sb[:, u * P:(u + 1) * P], w_sb[:, 0, :],
                                            start=True, stop=True)
                last.then_inc(s_y, 1)

            def step(g, coming, before, earlier, nxt):
                after = coming[0]
                units = list(after.units) if after else []
                of = max(2, len(units))
                for n in range(of):
                    if n < len(units):
                        transpose_unit(after, units[n])
                    products(g, n, of)
                    if n == PROJ and before:
                        project(before)
                if after is None:
                    pe.wait_ge(s_found, 1)
                    nc.tensor.matmul(ids_t[0][0:1, 0, 0:2].bitcast(FP32), found[:, :], ones[:, :],
                                     start=True, stop=True).then_inc(s_count, 1)
                    project(g)

            pe.wait_ge(s_ident, 1)
            start = Batch(0, 0, 0, STEADY, NG)
            for u in start.groups[0].units:
                transpose_unit(start.groups[0], u)
            pe.wait_ge(s_w, 16)
            walk(pe, step)

        @block.vector
        def _(dve):
            def scale_maxima(batch):
                dve.wait_ge(s_x[batch.side], 16 * (batch.turn + 1))
                nc.vector.tensor_reduce(row_max[:, :], x_sb[:, batch.side], AX.X, ALU.max,
                                        apply_absolute_value=True).then_inc(s_rm, 1)

            def scale_largest(batch):
                dve.wait_ge(s_rm, batch.b + 1)
                nc.vector.tensor_reduce(largest[:, :], row_max[:, :], AX.X, ALU.max).then_inc(s_mx, 1)

            def scale_power(batch):
                dve.wait_ge(s_mx, batch.b + 1)
                nc.vector.tensor_scalar(power[:, :].bitcast(INT32), largest[:, :].bitcast(INT32), EXPONENT, None,
                                        ALU.bitwise_and).then_inc(s_pw, 1)
                nc.vector.tensor_scalar(far[:, :], row_max[:, :], SPAN, largest[:, :], ALU.mult, ALU.is_lt).then_inc(s_far, 1)

            def scale_down(batch):
                dve.wait_ge(s_pw, batch.b + 1)
                s = slice(batch.side, batch.side + 1)
                nc.vector.tensor_scalar(down[:, s], power[:, :], LEAST, 2.0 ** -TOP, ALU.max, ALU.mult).then_inc(s_dn, 1)

            def scale_up(batch):
                dve.wait_ge(s_far, batch.b + 1)
                nc.vector.scalar_tensor_tensor(out=far[:, :], in0=row_max[:, :], scalar=0.0, in1=far[:, :],
                                               op0=ALU.is_gt, op1=ALU.mult).then_inc(s_far2, 1)
                dve.wait_ge(s_dn, batch.b + 1)
                s = slice(batch.side, batch.side + 1)
                nc.vector.reciprocal(up[:, s], down[:, s]).then_inc(s_scale, 1)

            def scale_unsuited(batch):
                dve.wait_ge(s_far2, batch.b + 1)
                nc.vector.tensor_tensor(unsuited[:, :], unsuited[:, :], far[:, :], ALU.max).then_inc(s_uns, 1)

            def mask_unit(g, u):
                dve.wait_ge(s_tr, unit_no(g, u) + 1)
                if not is_first(g.batch):
                    dve.wait_ge(s_prod, group_of(g, u) + 1)
                side = g.batch.side
                nc.vector.tensor_scalar(mask_t[:, :, u * P:(u + 1) * P], ids_t[u % T_BANKS][:, :, :],
                                        down[:, side:side + 1], None, ALU.mult, ALU.max,
                                        accum_out=peak[:, side, u:u + 1]).then_inc(s_mask, 1)

            def compare(batch):
                dve.wait_ge(s_mask, J * (batch.b + 1))
                if not is_first(batch):
                    dve.wait_ge(s_cmp, batch.b)
                nc.vector.scalar_tensor_tensor(out=excess[:, :], in0=peak[:, batch.side], scalar=down[:, batch.side:batch.side + 1],
                                               in1=excess[:, :], op0=ALU.subtract, op1=ALU.max).then_inc(s_cmp, 1)

            def sum_rows(g):
                dve.wait_ge(s_y, g.index + 1)
                dve.wait_ge(s_xb, g.batch.b + 1)
                dve.wait_ge(s_out[g.batch.side][g.units[-1] // GU], 16 * g.batch.turn + 1)
                us = slice(g.first, g.first + g.count)
                nc.vector.tensor_tensor(rows[:, g.batch.side, us, :], y_ps[g.bank][:, 0:g.count, :], xb[:, g.batch.side, us, :],
                                        ALU.add).then_inc(s_sum, 1)

            def statistics(g):
                dve.wait_ge(s_sum, g.index + 2)
                for u in g.units:
                    last = nc.vector.bn_stats(stats[:, u, :], rows[:, g.batch.side, u, :])
                last.then_inc(s_st, 1)

            def combine(g):
                dve.wait_ge(s_st, g.index + 1)
                us = slice(g.first, g.first + g.count)
                even, odd = stats[:, us, 0:3], stats[:, us, 3:6]
                nc.vector.tensor_tensor(gap[:, us], even[:, :, 1], odd[:, :, 1], ALU.subtract).then_inc(s_gap, 1)
                nc.vector.tensor_tensor(mean2[:, us], even[:, :, 1], odd[:, :, 1], ALU.add)
                nc.vector.tensor_tensor(within[:, us], even[:, :, 2], odd[:, :, 2], ALU.add).then_inc(s_within, 1)
                dve.wait_ge(s_gap, g.index + 1)
                nc.vector.tensor_tensor(gap[:, us], gap[:, us], gap[:, us], ALU.mult).then_inc(s_gap2, 1)

            def variances(g):
                dve.wait_ge(s_gap2, g.index + 1)
                dve.wait_ge(s_within, g.index + 1)
                us = slice(g.first, g.first + g.count)
                nc.vector.scalar_tensor_tensor(out=spread[:, us], in0=gap[:, us], scalar=D / 4.0, in1=within[:, us],
                                               op0=ALU.mult, op1=ALU.add).then_inc(s_var, 1)

            def invert(g):
                dve.wait_ge(s_std, g.index + 1)
                us = slice(g.first, g.first + g.count)
                nc.vector.reciprocal(guess[:, us], std[:, us]).then_inc(s_n[0], 1)

            def newton_square(g):
                dve.wait_ge(s_n[0], g.index + 1)
                us = slice(g.first, g.first + g.count)
                nc.vector.tensor_tensor(square[:, us], guess[:, us], guess[:, us], ALU.mult).then_inc(s_n[1], 1)

            def newton_product(g):
                dve.wait_ge(s_n[1], g.index + 1)
                us = slice(g.first, g.first + g.count)
                nc.vector.scalar_tensor_tensor(out=half[:, us], in0=spread[:, us], scalar=D * EPS,
                                               in1=square[:, us], op0=ALU.add, op1=ALU.mult).then_inc(s_n[2], 1)

            def newton_factor(g):
                dve.wait_ge(s_n[2], g.index + 1)
                us = slice(g.first, g.first + g.count)
                nc.vector.tensor_scalar(square[:, us], half[:, us], -0.5 / D, 1.5, ALU.mult, ALU.add).then_inc(s_n[3], 1)

            def newton_result(g):
                dve.wait_ge(s_n[3], g.index + 1)
                us = slice(g.first, g.first + g.count)
                nc.vector.tensor_tensor(rstd[:, us], guess[:, us], square[:, us], ALU.mult).then_inc(s_n[4], 1)

            def make_shift(g):
                dve.wait_ge(s_n[4], g.index + 1)
                us = slice(g.first, g.first + g.count)
                nc.vector.scalar_tensor_tensor(out=shift[:, us], in0=mean2[:, us], scalar=-0.5,
                                               in1=rstd[:, us], op0=ALU.mult, op1=ALU.mult).then_inc(s_rstd, 1)

            def invert_root(g):
                invert(g)
                newton_square(g)
                newton_product(g)
                newton_factor(g)
                newton_result(g)
                make_shift(g)

            def step(g, coming, before, earlier, nxt):
                after = coming[0]
                due = list(after.units) if after else []
                ready = nxt if g.place == 0 else None

                def do(part, what):
                    if what:
                        part(what)

                def mask_next():
                    if due:
                        mask_unit(after, due.pop(0))

                mask_next()
                do(invert, earlier)
                do(scale_maxima, ready)
                do(newton_square, earlier)
                do(scale_largest, ready)
                mask_next()
                do(newton_product, earlier)
                do(scale_power, ready)
                do(newton_factor, earlier)
                do(scale_down, ready)
                do(newton_result, earlier)
                mask_next()
                do(make_shift, earlier)
                do(scale_up, ready)
                do(sum_rows, before)
                mask_next()
                do(scale_unsuited, ready)
                do(statistics, before)
                do(combine, before)
                do(variances, before)
                if after is not None and after.batch is g.batch and after.place == len(g.batch.groups) - 1:
                    compare(g.batch)
                if after is None:
                    dve.wait_ge(s_cmp, B)
                    nc.vector.tensor_tensor(excess[:, :], excess[:, :], unsuited[:, :], ALU.max).then_inc(s_both, 1)
                    dve.wait_ge(s_both, 1)
                    nc.vector.tensor_reduce(worst[:, :], excess[:, :], AX.X, ALU.max).then_inc(s_worst, 1)
                    dve.wait_ge(s_worst, 1)
                    nc.vector.tensor_scalar(found[:, :], worst[:, :], 0.0, None, ALU.is_gt).then_inc(s_found, 1)
                    dve.wait_ge(s_count, 1)
                    nc.vector.tensor_copy(again[:, :], ids_t[0][0:1, 0, 0:2].bitcast(FP32)).then_inc(s_again, 1)
                    invert_root(before)
                    sum_rows(g)
                    statistics(g)
                    combine(g)
                    variances(g)
                    invert_root(g)

            s_rm, s_mx, s_pw, s_dn = (sem(n) for n in ("row_max_ready", "largest_ready", "power_ready", "down_ready"))
            s_far, s_far2, s_uns, s_both = (sem(n) for n in ("far_ready", "far_nonzero", "unsuited_ready", "both_ready"))
            s_st = sem("stats_ready")
            s_gap, s_gap2, s_within = (sem(n) for n in ("gap_ready", "gap_squared", "within_ready"))
            s_cmp = sem("batches_compared")
            s_worst = sem("worst_ready")
            s_n = [sem(f"newton{n}") for n in range(5)]
            nc.vector.memset(eps[:, :], EPS)
            nc.vector.memset(ones[:, :], 1.0)
            nc.vector.memset(excess[:, :], 0.0)
            nc.vector.memset(unsuited[:, :], 0.0).then_inc(s_const, 1)
            dve.wait_ge(s_const, 1)
            dve.sem_inc(s_sum, 1)
            start = Batch(0, 0, 0, STEADY, NG)
            for part in (scale_maxima, scale_largest, scale_power, scale_down, scale_up, scale_unsuited):
                part(start)
            mask_unit(start.groups[0], 0)
            for u in start.groups[0].units[1:]:
                mask_unit(start.groups[0], u)
            walk(dve, step)

        first_pass.close()

        g_w = sem("g_weights_loaded")
        g_x = sem("g_x_loaded")
        g_adj = [sem(f"g_adj_loaded{n}") for n in range(PAIRS)]
        g_out, g_batch = sem("g_rows_stored"), sem("g_batches_stored")
        g_hi, g_rest, g_mid, g_lo, g_xb = (sem(f"g_{n}_ready") for n in ("hi", "rest", "mid", "lo", "xb"))
        g_cast, g_tr, g_mask = sem("g_units_cast"), sem("g_units_transposed"), sem("g_units_masked")
        g_prod, g_h, g_y = sem("g_products_done"), sem("g_h_copied"), sem("g_projected")
        g_sum, g_stats, g_gap, g_var = sem("g_summed"), sem("g_stats"), sem("g_gap"), sem("g_var")
        g_std, g_norm = sem("g_std"), sem("g_normalised")
        g_newton = [sem(f"g_newton{n}") for n in range(6)]
        g_gap2 = sem("g_gap_squared")

        parts = [x_hi[:, 0].bitcast(BF16), x_hi[:, 1].bitcast(BF16), x_lo[:, 0].bitcast(BF16)]
        rest = xb[:, 1]

        def halves(t, n):
            return t[..., n * GU * P:(n + 1) * GU * P]

        def second_pass():
            with nc.Block() as block:
                @block.sync
                def _(sp):
                    sp.dma_start(w_sb[:, 1:R, :], weight[1:R].rearrange("r d o -> d r o")).then_inc(g_w, 16)
                    with sp.Fori(0, B) as b:
                        sp.dma_start(x_sb[:, 0], x_d[b]).then_inc(g_x, 16)
                        for k in range(PAIRS):
                            sp.dma_start(adj_sb[:, 0, 2 * k:2 * k + 2, :],
                                         adj_d[b, :, 2 * k:2 * k + 2, :]).then_inc(g_adj[k], 16)
                        for g in range(NG):
                            sp.wait_ge(g_norm, NG * b + g + 1)
                            sp.dma_start(out_d[b, :, g * GU:(g + 1) * GU, :],
                                         rows[:, 0, g * GU:(g + 1) * GU, :]).then_inc(g_out, 16)
                        sp.wait_ge(g_out, 16 * NG * (b + 1))
                        sp.sem_inc(g_batch, 1)

                @block.gpsimd
                def _(pool):
                    with pool.Fori(0, B) as b:
                        pool.wait_ge(g_x, 16 * (b + 1))
                        nc.gpsimd.tensor_tensor(xb[:, 0], x_sb[:, 0],
                                                bias_sb[:, :].unsqueeze(1).to_broadcast([P, J, D]),
                                                ALU.add).then_inc(g_xb, 1)

                @block.scalar
                def _(act):
                    with act.Fori(0, B) as b:
                        for u in range(J):
                            act.wait_ge(g_adj[u // 2], 16 * (b + 1))
                            nc.scalar.activation(ids[:, u], adj_sb[:, 0, u, :].rearrange("p (q j) -> p j q", j=J),
                                                 ACT.Relu).then_inc(g_cast, 1)
                        act.wait_ge(g_x, 16 * (b + 1))
                        nc.scalar.activation(parts[0], x_sb[:, 0], ACT.Copy).then_inc(g_hi, 1)
                        for g in range(NG):
                            for r in range(R):
                                done = R * (NG * b + g) + r
                                act.wait_ge(g_prod, done + 1)
                                nc.scalar.activation(h_all[:, r, :], h_ps[r % 2][:, :], ACT.Copy).then_inc(g_h, 1)
                            act.wait_ge(g_var, NG * b + g + 1)
                            us = slice(g * GU, (g + 1) * GU)
                            nc.scalar.activation(std[:, us], spread[:, us], ACT.Sqrt, bias=eps[:, 0:1],
                                                 scale=1.0 / D).then_inc(g_std, 1)

                @block.tensor
                def _(pe):
                    pe.wait_ge(g_w, 16)
                    with pe.Fori(0, B) as b:
                        for g in range(NG):
                            for n in range(GU):
                                pe.wait_ge(g_cast, J * b + GU * g + n + 1)
                                if g:
                                    pe.wait_ge(g_mask, R * GU * (NG * b + g))
                                for j in range(J):
                                    last = nc.tensor.transpose(ids_t[n][:, j, :], ids[:, g * GU + n, j, :], ident[:, :])
                                last.then_inc(g_tr, 1)
                            pe.wait_ge(g_hi, b + 1)
                            pe.wait_ge(g_lo, b + 1)
                            for r in range(R):
                                done = R * (NG * b + g) + r
                                pe.wait_ge(g_mask, GU * (done + 1))
                                if r >= 2:
                                    pe.wait_ge(g_h, done - 1)
                                for j in range(J):
                                    for n, part in enumerate(parts):
                                        last = nc.tensor.matmul(
                                            h_ps[r % 2][:, :], part[:, j, :], halves(mask_t[:, j, :], r % 2),
                                            start=(j == 0 and n == 0), stop=(j == J - 1 and n == len(parts) - 1))
                                last.then_inc(g_prod, 1)
                            pe.wait_ge(g_h, R * (NG * b + g + 1))
                            for n in range(GU):
                                for r in range(R):
                                    last = nc.tensor.matmul(y_ps[0][:, n, :], h_all[:, r, n * P:(n + 1) * P],
                                                            w_sb[:, r, :], start=(r == 0), stop=(r == R - 1))
                            last.then_inc(g_y, 1)

                @block.vector
                def _(dve):
                    with dve.Fori(0, B) as b:
                        dve.wait_ge(g_hi, b + 1)
                        nc.vector.tensor_tensor(rest, x_sb[:, 0], parts[0], ALU.subtract).then_inc(g_rest, 1)
                        dve.wait_ge(g_rest, b + 1)
                        nc.vector.tensor_copy(parts[1], rest).then_inc(g_mid, 1)
                        dve.wait_ge(g_mid, b + 1)
                        nc.vector.tensor_tensor(parts[2], rest, parts[1], ALU.subtract).then_inc(g_lo, 1)
                        for g in range(NG):
                            us = slice(g * GU, (g + 1) * GU)
                            for r in range(R):
                                if r >= 2:
                                    dve.wait_ge(g_prod, R * (NG * b + g) + r - 1)
                                for n in range(GU):
                                    dve.wait_ge(g_tr, J * b + GU * g + n + 1)
                                    at = (r % 2 * GU + n) * P
                                    nc.vector.tensor_scalar(mask_t[:, :, at:at + P], ids_t[n][:, :, :], float(r + 1),
                                                            None, ALU.is_equal).then_inc(g_mask, 1)
                            dve.wait_ge(g_xb, b + 1)
                            dve.wait_ge(g_y, NG * b + g + 1)
                            nc.vector.tensor_tensor(rows[:, 0, us, :], y_ps[0][:, :, :], xb[:, 0, us, :], ALU.add).then_inc(g_sum, 1)
                            dve.wait_ge(g_sum, NG * b + g + 1)
                            for u in range(g * GU, (g + 1) * GU):
                                last = nc.vector.bn_stats(stats[:, u, :], rows[:, 0, u, :])
                            last.then_inc(g_stats, 1)
                            dve.wait_ge(g_stats, NG * b + g + 1)
                            even, odd = stats[:, us, 0:3], stats[:, us, 3:6]
                            nc.vector.tensor_tensor(gap[:, us], even[:, :, 1], odd[:, :, 1], ALU.subtract)
                            nc.vector.tensor_tensor(mean2[:, us], even[:, :, 1], odd[:, :, 1], ALU.add)
                            nc.vector.tensor_tensor(within[:, us], even[:, :, 2], odd[:, :, 2], ALU.add).then_inc(g_gap, 1)
                            dve.wait_ge(g_gap, NG * b + g + 1)
                            nc.vector.tensor_tensor(gap[:, us], gap[:, us], gap[:, us], ALU.mult).then_inc(g_gap2, 1)
                            dve.wait_ge(g_gap2, NG * b + g + 1)
                            nc.vector.scalar_tensor_tensor(out=spread[:, us], in0=gap[:, us], scalar=D / 4.0,
                                                           in1=within[:, us], op0=ALU.mult, op1=ALU.add).then_inc(g_var, 1)
                            dve.wait_ge(g_std, NG * b + g + 1)
                            nc.vector.reciprocal(guess[:, us], std[:, us]).then_inc(g_newton[0], 1)
                            dve.wait_ge(g_newton[0], NG * b + g + 1)
                            nc.vector.tensor_tensor(square[:, us], guess[:, us], guess[:, us], ALU.mult).then_inc(g_newton[1], 1)
                            dve.wait_ge(g_newton[1], NG * b + g + 1)
                            nc.vector.scalar_tensor_tensor(out=half[:, us], in0=spread[:, us], scalar=D * EPS,
                                                           in1=square[:, us], op0=ALU.add, op1=ALU.mult).then_inc(g_newton[2], 1)
                            dve.wait_ge(g_newton[2], NG * b + g + 1)
                            nc.vector.tensor_scalar(square[:, us], half[:, us], -0.5 / D, 1.5, ALU.mult, ALU.add).then_inc(g_newton[3], 1)
                            dve.wait_ge(g_newton[3], NG * b + g + 1)
                            nc.vector.tensor_tensor(rstd[:, us], guess[:, us], square[:, us], ALU.mult).then_inc(g_newton[4], 1)
                            dve.wait_ge(g_newton[4], NG * b + g + 1)
                            nc.vector.scalar_tensor_tensor(out=shift[:, us], in0=mean2[:, us], scalar=-0.5,
                                                           in1=rstd[:, us], op0=ALU.mult, op1=ALU.mult).then_inc(g_newton[5], 1)
                            dve.wait_ge(g_newton[5], NG * b + g + 1)
                            for u in range(g * GU, (g + 1) * GU):
                                last = nc.vector.tensor_scalar(rows[:, 0, u, :], rows[:, 0, u, :], rstd[:, u:u + 1],
                                                               shift[:, u:u + 1], ALU.mult, ALU.add)
                            last.then_inc(g_norm, 1)

        high = nc.values_load(again[0:1, 0:1], min_val=0, max_val=P)
        with nc.If(high > 0):
            second_pass()


def kernel(x, adj, L0_gnn_adj, L0_gnn_weight, L0_gnn_bias):
    import numpy as np
    import concourse.bacc as bacc
    from concourse.bass_utils import run_bass_kernel_spmd

    nc = bacc.Bacc("TRN2", target_bir_lowering=False, num_devices=1)
    arrays = {"x": np.ascontiguousarray(x), "adj": np.ascontiguousarray(adj),
              "weight": np.ascontiguousarray(L0_gnn_weight), "bias": np.ascontiguousarray(L0_gnn_bias)}
    args = [nc.dram_tensor(name, a.shape, mybir.dt.from_np(a.dtype), kind="ExternalInput").ap()
            for name, a in arrays.items()]
    out = nc.dram_tensor("out", arrays["x"].shape, FP32, kind="ExternalOutput").ap()
    adj_resnorm_kernel(nc, *args, out)
    return run_bass_kernel_spmd(nc, [arrays], core_ids=[0]).results[0]["out"]
```

```python
from contextlib import ExitStack

import concourse.bass as bass
from concourse import mybir

P = 128
FP32 = mybir.dt.float32
BF16 = mybir.dt.bfloat16
FP16 = mybir.dt.float16
INT32 = mybir.dt.int32
ALU = mybir.AluOpType
ACT = mybir.ActivationFunctionType
AX = mybir.AxisListType
EPS = 1e-5
TOP = 14
SPAN = 2.0 ** 14
LEAST = 2.0 ** -100
EXPONENT = 0x7F800000


class Group:

    def __init__(self, batch, place, first, count):
        self.batch, self.place, self.first, self.count = batch, place, first, count
        self.index = batch.first_group + place
        self.bank = place % 2
        self.units = range(first, first + count)
        self.cols = slice(first * P, (first + count) * P)


class Batch:

    def __init__(self, b, side, turn, shape, per_batch):
        self.b, self.side, self.turn = b, side, turn
        self.first_group = per_batch * b
        self.groups = [Group(self, n, f, c) for n, (f, c) in enumerate(shape)]


def adj_resnorm_kernel(nc, x, adj, weight, bias, out):
    B, N, D = x.shape
    R = weight.shape[0]
    J = N // P
    PAIRS = J // 2
    GU = 4
    STEADY = [(f, GU) for f in range(0, J, GU)]
    FINAL = [(0, 4), (4, 2), (6, 2)]
    NG = len(STEADY)
    T_BANKS = 4
    AHEAD = 2
    LATER = 4
    assert J == 8 and R > 1 and B % 2 == 0 and B >= 6 and FINAL[0] == STEADY[0]

    x_d = x.rearrange("b (p j) d -> b p j d", j=J)
    adj_d = adj.rearrange("b (p j) m -> b p j m", j=J)
    out_d = out.rearrange("b (p j) d -> b p j d", j=J)

    ctx = ExitStack()
    with ctx:
        def sb(name, shape, dt):
            return ctx.enter_context(nc.sbuf_tensor(name, shape, dt))

        def pb(name, shape, dt):
            return ctx.enter_context(nc.psum_tensor(name, shape, dt))

        def sem(name):
            return ctx.enter_context(nc.semaphore(name))

        ident = sb("ident", [P, P], BF16)
        ones = sb("ones", [P, 1], FP32)
        eps = sb("eps", [P, 1], FP32)
        bias_sb = sb("bias_sb", [P, D], FP32)
        w_sb = sb("w_sb", [P, R, D], FP32)
        adj_sb = sb("adj_sb", [P, 2, J, N], INT32)
        ids = sb("ids", [P, J, J, P], BF16)
        mask_t = sb("mask_t", [P, J, N], BF16)
        x_sb = sb("x_sb", [P, 2, J, D], FP32)
        x_up = sb("x_up", [P, J, D], FP32)
        x_hi = sb("x_hi", [P, 2, J, D], FP16)
        x_lo = sb("x_lo", [P, 2, J, D], FP16)
        xb = sb("xb", [P, 2, J, D], FP32)
        row_max = sb("row_max", [P, J], FP32)
        largest = sb("largest", [P, 1], FP32)
        power = sb("power", [P, 1], FP32)
        down = sb("down", [P, 2], FP32)
        up = sb("up", [P, 2], FP32)
        h_all = sb("h_all", [P, R, GU * P], FP32)
        h_sb = h_all[:, 0:N // (GU * P), :].rearrange("p r n -> p (r n)")
        rows = sb("rows", [P, 2, J, D], FP32)
        stats = sb("stats", [P, J, 6], FP32)
        gap = sb("gap", [P, J], FP32)
        within = sb("within", [P, J], FP32)
        mean2 = sb("mean2", [P, J], FP32)
        spread = sb("spread", [P, J], FP32)
        std = sb("std", [P, J], FP32)
        guess = sb("guess", [P, J], FP32)
        square = sb("square", [P, J], FP32)
        half = sb("half", [P, J], FP32)
        rstd = sb("rstd", [P, 2, J], FP32)
        shift = sb("shift", [P, 2, J], FP32)
        far = sb("far", [P, J], FP32)
        unsuited = sb("unsuited", [P, J], FP32)
        peak = sb("peak", [P, 2, J], FP32)
        excess = sb("excess", [P, J], FP32)
        worst = sb("worst", [P, 1], FP32)
        found = sb("found", [P, 1], FP32)
        again = sb("again", [1, 1], INT32)

        ids_t = [pb(f"ids_t{n}", [P, J, P], BF16) for n in range(T_BANKS)]
        h_ps = [pb(f"h_ps{n}", [P, GU * P], FP32) for n in range(2)]
        y_ps = [pb(f"y_ps{n}", [P, GU, D], FP32) for n in range(2)]

        s_w = sem("weights_loaded")
        s_bias = sem("bias_loaded")
        s_x = [sem(f"x_loaded{n}") for n in range(2)]
        s_adj = [[sem(f"adj_loaded{side}{n}") for n in range(PAIRS)] for side in range(2)]
        s_out = [[sem(f"rows_stored{side}{n}") for n in range(NG)] for side in range(2)]
        s_last = sem("last_rows_stored")
        s_zero = sem("ident_zeroed")
        s_ident = sem("ident_ready")
        s_const = sem("constants_ready")
        s_cast = sem("units_cast")
        s_tr = sem("units_transposed")
        s_mask = sem("units_masked")
        s_scale = sem("batches_scaled")
        s_up = sem("x_scaled")
        s_hi = sem("hi_ready")
        s_lo = sem("lo_ready")
        s_xb = sem("xb_ready")
        s_prod = sem("groups_multiplied")
        s_h = sem("h_copied")
        s_y = sem("groups_projected")
        s_sum = sem("groups_summed")
        s_var = sem("variances_ready")
        s_std = sem("std_ready")
        s_rstd = sem("rstd_ready")
        s_half = sem("rows_times_rstd")
        s_norm = sem("groups_normalised")
        s_aside = sem("last_rows_normalised_by_act")
        s_done = sem("last_rows_normalised_by_dve")
        s_found = sem("found_ready")
        s_count = sem("count_ready")
        s_again = sem("again_ready")

        def walk(eng, step, finish, ahead=1, behind=1):
            def one(cur, nxt, prev):
                past = [None, None] if prev is None else prev.groups[-2:]
                order = past + cur.groups + (nxt.groups if nxt else []) + [None, None]
                for n, g in enumerate(cur.groups):
                    step(g, order[n + 3:n + 5], order[n + 1], order[n], nxt)

            def fixed(b):
                return Batch(b, b % 2, b // 2, FINAL if b == B - 1 else STEADY, NG) if 0 <= b < B else None

            def turning(i, n):
                n += ahead
                return Batch(2 * i + n, n % 2, i + n // 2, STEADY, NG)

            for b in range(ahead):
                one(fixed(b), fixed(b + 1), fixed(b - 1))
            with eng.Fori(0, (B - ahead - behind) // 2) as i:
                for n in range(2):
                    one(turning(i, n), turning(i, n + 1), turning(i, n - 1))
            for b in range(B - behind, B - 1):
                one(fixed(b), fixed(b + 1), fixed(b - 1))
            finish(*(fixed(B - 3).groups + fixed(B - 2).groups)[-3:], *fixed(B - 1).groups)

        def joined(b, c):
            return Group(b.batch, b.place, b.first, b.count + c.count)

        def three_before(g):
            batch = g.batch
            if isinstance(batch.b, int) and NG * batch.b + g.place < 3:
                return None
            if g.place > 0:
                return Batch(batch.b - 1, 1 - batch.side, batch.turn - 1 + batch.side, STEADY, NG).groups[g.place - 1]
            return Batch(batch.b - 2, batch.side, batch.turn - 1, STEADY, NG).groups[1]

        def unit_no(g, u):
            return J * g.batch.b + u

        def group_of(g, u):
            return NG * (g.batch.b - 1) + u // GU

        def is_first(batch):
            return isinstance(batch.b, int) and batch.b == 0

        first_pass = ExitStack()
        block = first_pass.enter_context(nc.Block())

        @block.sync
        def _(sp):
            def load_x(batch):
                if not (isinstance(batch.b, int) and batch.b < 2):
                    sp.wait_ge(s_up, batch.b - 1)
                    sp.wait_ge(s_hi, batch.b - 1)
                    sp.wait_ge(s_xb, batch.b - 1)
                sp.dma_start(x_sb[:, batch.side], x_d[batch.b]).then_inc(s_x[batch.side], 16)

            def load_adj(batch, k):
                if not (isinstance(batch.b, int) and batch.b < 2):
                    sp.wait_ge(s_cast, J * (batch.b - 2) + 2 * k + 2 + LATER)
                sp.dma_start(adj_sb[:, batch.side, 2 * k:2 * k + 2, :],
                             adj_d[batch.b, :, 2 * k:2 * k + 2, :]).then_inc(s_adj[batch.side][k], 16)

            def step(g, coming, before, earlier, nxt):
                b, side, turn = g.batch.b, g.batch.side, g.batch.turn
                if not (isinstance(b, int) and b + 2 >= B):
                    if g.place == NG - 1 and not (isinstance(b, int) and b + 3 >= B):
                        load_x(Batch(b + 3, 1 - side, turn + 1 + side, STEADY, NG))
                    for k in range(PAIRS // NG * g.place, PAIRS // NG * (g.place + 1)):
                        load_adj(Batch(b + 2, side, turn + 1, STEADY, NG), k)

            for side in range(2):
                for n in range(NG):
                    sp.sem_inc(s_out[side][n], 1)
            first, second = (Batch(n, n, 0, STEADY, NG) for n in range(2))
            load_x(first)
            load_adj(first, 0)
            sp.dma_start(w_sb[:, 0, :], weight[0]).then_inc(s_w, 16)
            sp.dma_start(bias_sb[:, :], bias.rearrange("(a d) -> a d", a=1).to_broadcast([P, D])).then_inc(s_bias, 16)
            load_adj(first, 1)
            load_x(second)
            load_adj(first, 2)
            load_adj(first, 3)
            load_adj(second, 0)
            load_adj(second, 1)
            load_x(Batch(2, 0, 1, STEADY, NG))
            load_adj(second, 2)
            load_adj(second, 3)

            def finish(oldest, older, old, a, b, c):
                both = joined(b, c)
                for g in (oldest, older, old, a, both):
                    if g is not both:
                        sp.wait_ge(s_norm, g.index + 1)
                    if g is a:
                        sp.wait_ge(s_aside, 1)
                    if g is both:
                        sp.wait_ge(s_aside, 2)
                        sp.wait_ge(s_done, 1)
                    sp.dma_start(out_d[g.batch.b, :, g.first:g.first + g.count, :],
                                 rows[:, g.batch.side, g.first:g.first + g.count, :]).then_inc(
                                     s_out[g.batch.side][g.place] if g is oldest else s_last, 16)

            walk(sp, step, finish, behind=3)
            early = range(NG * (B - 1) - 2)
            stored = [[sum(i // NG % 2 == side and i % NG == n for i in early) for n in range(NG)] for side in range(2)]
            for side in range(2):
                for n in range(NG):
                    sp.wait_ge(s_out[side][n], 16 * stored[side][n] + 1)
            sp.wait_ge(s_last, 16 * 4)

        @block.gpsimd
        def _(pool):
            nc.gpsimd.memset(ident[:, :], 0.0).then_inc(s_zero, 1)
            pool.wait_ge(s_zero, 1)
            nc.gpsimd.affine_select(out=ident[:, :], in_=ident[:, :], compare_op=ALU.not_equal, fill=1.0,
                                    base=0, pattern=[[-1, P]], channel_multiplier=1).then_inc(s_ident, 1)

            def add_bias(batch):
                pool.wait_ge(s_x[batch.side], 16 * (batch.turn + 1))
                if not (isinstance(batch.b, int) and batch.b < 2):
                    pool.wait_ge(s_sum, NG * (batch.b - 1) + 1)
                nc.gpsimd.tensor_tensor(xb[:, batch.side], x_sb[:, batch.side],
                                        bias_sb[:, :].unsqueeze(1).to_broadcast([P, J, D]),
                                        ALU.add).then_inc(s_xb, 1)

            def scale_x(batch):
                pool.wait_ge(s_scale, batch.b + 1)
                if not is_first(batch):
                    pool.wait_ge(s_lo, batch.b)
                nc.gpsimd.tensor_tensor(x_up[:, :], x_sb[:, batch.side],
                                        up[:, batch.side:batch.side + 1].unsqueeze(2).to_broadcast([P, J, D]),
                                        ALU.mult).then_inc(s_up, 1)

            def split_lo(batch):
                pool.wait_ge(s_up, batch.b + 1)
                pool.wait_ge(s_hi, batch.b + 1)
                if not (isinstance(batch.b, int) and batch.b < 2):
                    pool.wait_ge(s_prod, NG * (batch.b - 1))
                nc.gpsimd.tensor_tensor(x_lo[:, batch.side], x_up[:, :], x_hi[:, batch.side],
                                        ALU.subtract).then_inc(s_lo, 1)

            def normalise(g):
                pool.wait_ge(s_rstd, g.index + 1)
                part = rows[:, g.batch.side, g.first:g.first + g.count, :]
                wide = [P, g.count, D]
                nc.gpsimd.tensor_tensor(part, part, rstd[:, g.batch.side, g.first:g.first + g.count].unsqueeze(2).to_broadcast(wide),
                                        ALU.mult).then_inc(s_half, 1)
                pool.wait_ge(s_half, g.index + 1)
                nc.gpsimd.tensor_tensor(part, part, shift[:, g.batch.side, g.first:g.first + g.count].unsqueeze(2).to_broadcast(wide),
                                        ALU.add).then_inc(s_norm, 1)

            def step(g, coming, before, earlier, nxt):
                if earlier:
                    normalise(earlier)
                if g.place == 0 and nxt is not None:
                    scale_x(nxt)
                    split_lo(nxt)
                if g.place == NG - 1 and nxt is not None:
                    add_bias(nxt)

            def finish(oldest, older, old, a, b, c):
                normalise(older)
                normalise(old)
                normalise(Group(a.batch, a.place, a.first, 2))

            scale_x(Batch(0, 0, 0, STEADY, NG))
            split_lo(Batch(0, 0, 0, STEADY, NG))
            pool.wait_ge(s_bias, 16)
            add_bias(Batch(0, 0, 0, STEADY, NG))
            walk(pool, step, finish)

        @block.scalar
        def _(act):
            def cast(batch, u):
                act.wait_ge(s_adj[batch.side][u // 2], 16 * (batch.turn + 1))
                if not is_first(batch):
                    act.wait_ge(s_tr, J * (batch.b - 1) + u + 1)
                nc.scalar.activation(ids[:, u], adj_sb[:, batch.side, u, :].rearrange("p (q j) -> p j q", j=J),
                                     ACT.Relu).then_inc(s_cast, 1)

            def split_hi(batch):
                act.wait_ge(s_scale, batch.b + 1)
                if not (isinstance(batch.b, int) and batch.b < 2):
                    act.wait_ge(s_prod, NG * (batch.b - 1))
                nc.scalar.activation(x_hi[:, batch.side], x_sb[:, batch.side], ACT.Copy,
                                     scale=up[:, batch.side:batch.side + 1]).then_inc(s_hi, 1)

            def copy_h(g):
                act.wait_ge(s_prod, g.index + 1)
                nc.scalar.activation(h_sb[:, g.cols], h_ps[g.bank][:, 0:g.count * P], ACT.Copy).then_inc(s_h, 1)

            def root(g):
                act.wait_ge(s_var, g.index + 1)
                nc.scalar.activation(std[:, g.first:g.first + g.count], spread[:, g.first:g.first + g.count],
                                     ACT.Sqrt, bias=eps[:, 0:1]).then_inc(s_std, 1)

            def store(g):
                act.wait_ge(s_norm, g.index + 1)
                act.dma_start(out_d[g.batch.b, :, g.first:g.first + g.count, :],
                              rows[:, g.batch.side, g.first:g.first + g.count, :]).then_inc(s_out[g.batch.side][g.place], 16)

            def step(g, coming, before, earlier, nxt):
                after = coming[0]
                due = [(after.batch, u + AHEAD) for u in after.units] if after else []
                due = [(batch, u) if u < J else (nxt, u - J) for batch, u in due]
                due = [(batch, u) for batch, u in due if batch is not None]

                def cast_next():
                    if due:
                        cast(*due.pop(0))

                if before:
                    copy_h(before)
                if earlier:
                    root(earlier)
                if three_before(g):
                    store(three_before(g))
                for _ in range(GU):
                    cast_next()
                if g.place == 0 and nxt is not None:
                    split_hi(nxt)

            def normalise(g, units):
                act.wait_ge(s_rstd, g.index + 1)
                for u in units:
                    last = nc.scalar.activation(rows[:, g.batch.side, u, :], rows[:, g.batch.side, u, :], ACT.Identity,
                                                bias=shift[:, g.batch.side, u:u + 1], scale=rstd[:, g.batch.side, u:u + 1])
                last.then_inc(s_aside, 1)

            def finish(oldest, older, old, a, b, c):
                copy_h(old)
                cast(a.batch, GU + AHEAD)
                root(older)
                for u in range(GU + AHEAD + 1, J):
                    cast(a.batch, u)
                copy_h(a)
                root(old)
                copy_h(b)
                copy_h(c)
                root(a)
                root(joined(b, c))
                normalise(a, a.units[2:])
                normalise(joined(b, c), b.units)

            act.preload_act_table(ACT.Sqrt)
            act.wait_ge(s_const, 1)
            start = Batch(0, 0, 0, STEADY, NG)
            cast(start, 0)
            split_hi(start)
            for u in range(1, GU + AHEAD):
                cast(start, u)
            walk(act, step, finish, ahead=2, behind=2)

        @block.tensor
        def _(pe):
            def transpose_unit(g, u):
                pe.wait_ge(s_cast, unit_no(g, u) + 1)
                bank = ids_t[u % T_BANKS]
                if not (is_first(g.batch) and u < T_BANKS):
                    pe.wait_ge(s_mask, unit_no(g, u) - T_BANKS + 1)
                for j in range(J):
                    last = nc.tensor.transpose(bank[:, j, :], ids[:, u, j, :], ident[:, :])
                last.then_inc(s_tr, 1)

            def products(g, n, of):
                todo = [(j, part) for part in (x_hi, x_lo) for j in range(J)]
                lo, hi = len(todo) * n // of, len(todo) * (n + 1) // of
                if n == 0:
                    pe.wait_ge(s_mask, unit_no(g, g.units[-1]) + 1)
                    pe.wait_ge(s_hi, g.batch.b + 1)
                    if not (is_first(g.batch) and g.place < 2):
                        pe.wait_ge(s_h, g.index - 1)
                if lo <= J < hi:
                    pe.wait_ge(s_lo, g.batch.b + 1)
                for j, part in todo[lo:hi]:
                    last = nc.tensor.matmul(h_ps[g.bank][:, 0:g.count * P], part[:, g.batch.side, j, :],
                                            mask_t[:, j, g.cols], start=(j == 0 and part is x_hi),
                                            stop=(j == J - 1 and part is x_lo))
                if hi == len(todo):
                    last.then_inc(s_prod, 1)

            def project(g, copied=None):
                if not (is_first(g.batch) and g.place < 1):
                    pe.wait_ge(s_sum, g.index)
                for part in copied or (g,):
                    pe.wait_ge(s_h, part.index + 1)
                    for u in part.units:
                        last = nc.tensor.matmul(y_ps[g.bank][:, u - g.first, :], h_sb[:, u * P:(u + 1) * P], w_sb[:, 0, :],
                                                start=True, stop=True)
                last.then_inc(s_y, 1)

            def step(g, coming, before, earlier, nxt):
                after = coming[0]
                products(g, 0, GU)
                transpose_unit(after, after.units[0])
                products(g, 1, GU)
                transpose_unit(after, after.units[1])
                if before:
                    project(before)
                transpose_unit(after, after.units[2])
                products(g, 2, GU)
                transpose_unit(after, after.units[3])
                products(g, 3, GU)

            def finish(oldest, older, old, a, b, c):
                for n in range(GU):
                    transpose_unit(a, GU + n)
                    products(a, n, GU)
                    if n == 1:
                        project(old)
                products(b, 0, 1)
                project(a)
                products(c, 0, 1)
                project(joined(b, c), (b, c))
                pe.wait_ge(s_found, 1)
                nc.tensor.matmul(ids_t[0][0:1, 0, 0:2].bitcast(FP32), found[:, :], ones[:, :],
                                 start=True, stop=True).then_inc(s_count, 1)

            pe.wait_ge(s_ident, 1)
            start = Batch(0, 0, 0, STEADY, NG)
            for u in start.groups[0].units:
                transpose_unit(start.groups[0], u)
            pe.wait_ge(s_w, 16)
            walk(pe, step, finish)

        @block.vector
        def _(dve):
            def scale_maxima(batch):
                dve.wait_ge(s_x[batch.side], 16 * (batch.turn + 1))
                nc.vector.tensor_reduce(row_max[:, :], x_sb[:, batch.side], AX.X, ALU.max,
                                        apply_absolute_value=True).then_inc(s_rm, 1)

            def scale_largest(batch):
                dve.wait_ge(s_rm, batch.b + 1)
                nc.vector.tensor_reduce(largest[:, :], row_max[:, :], AX.X, ALU.max).then_inc(s_mx, 1)

            def scale_power(batch):
                dve.wait_ge(s_mx, batch.b + 1)
                nc.vector.tensor_scalar(power[:, :].bitcast(INT32), largest[:, :].bitcast(INT32), EXPONENT, None,
                                        ALU.bitwise_and).then_inc(s_pw, 1)
                nc.vector.tensor_scalar(far[:, :], row_max[:, :], SPAN, largest[:, :], ALU.mult, ALU.is_lt).then_inc(s_far, 1)

            def scale_down(batch):
                dve.wait_ge(s_pw, batch.b + 1)
                s = slice(batch.side, batch.side + 1)
                nc.vector.tensor_scalar(down[:, s], power[:, :], LEAST, 2.0 ** -TOP, ALU.max, ALU.mult).then_inc(s_dn, 1)

            def scale_up(batch):
                dve.wait_ge(s_far, batch.b + 1)
                nc.vector.scalar_tensor_tensor(out=far[:, :], in0=row_max[:, :], scalar=0.0, in1=far[:, :],
                                               op0=ALU.is_gt, op1=ALU.mult).then_inc(s_far2, 1)
                dve.wait_ge(s_dn, batch.b + 1)
                s = slice(batch.side, batch.side + 1)
                nc.vector.reciprocal(up[:, s], down[:, s]).then_inc(s_scale, 1)

            def scale_unsuited(batch):
                dve.wait_ge(s_far2, batch.b + 1)
                nc.vector.tensor_tensor(unsuited[:, :], unsuited[:, :], far[:, :], ALU.max).then_inc(s_uns, 1)

            def mask_unit(g, u):
                dve.wait_ge(s_tr, unit_no(g, u) + 1)
                if not is_first(g.batch):
                    dve.wait_ge(s_prod, group_of(g, u) + 1)
                side = g.batch.side
                nc.vector.tensor_scalar(mask_t[:, :, u * P:(u + 1) * P], ids_t[u % T_BANKS][:, :, :],
                                        down[:, side:side + 1], None, ALU.mult, ALU.max,
                                        accum_out=peak[:, side, u:u + 1]).then_inc(s_mask, 1)

            def compare(batch):
                dve.wait_ge(s_mask, J * (batch.b + 1))
                if not is_first(batch):
                    dve.wait_ge(s_cmp, batch.b)
                nc.vector.scalar_tensor_tensor(out=excess[:, :], in0=peak[:, batch.side], scalar=down[:, batch.side:batch.side + 1],
                                               in1=excess[:, :], op0=ALU.subtract, op1=ALU.max).then_inc(s_cmp, 1)

            def sum_rows(g):
                dve.wait_ge(s_y, g.index + 1)
                dve.wait_ge(s_xb, g.batch.b + 1)
                dve.wait_ge(s_out[g.batch.side][g.units[-1] // GU], 16 * g.batch.turn + 1)
                us = slice(g.first, g.first + g.count)
                nc.vector.tensor_tensor(rows[:, g.batch.side, us, :], y_ps[g.bank][:, 0:g.count, :], xb[:, g.batch.side, us, :],
                                        ALU.add).then_inc(s_sum, 1)

            def statistics(g):
                dve.wait_ge(s_sum, g.index + 2)
                for u in g.units:
                    last = nc.vector.bn_stats(stats[:, u, :], rows[:, g.batch.side, u, :])
                last.then_inc(s_st, 1)

            def combine(g):
                dve.wait_ge(s_st, g.index + 1)
                us = slice(g.first, g.first + g.count)
                even, odd = stats[:, us, 0:3], stats[:, us, 3:6]
                nc.vector.tensor_tensor(gap[:, us], even[:, :, 1], odd[:, :, 1], ALU.subtract).then_inc(s_gap, 1)
                nc.vector.tensor_tensor(mean2[:, us], even[:, :, 1], odd[:, :, 1], ALU.add)
                nc.vector.tensor_tensor(within[:, us], even[:, :, 2], odd[:, :, 2], ALU.add).then_inc(s_within, 1)
                dve.wait_ge(s_gap, g.index + 1)
                nc.vector.tensor_tensor(gap[:, us], gap[:, us], gap[:, us], ALU.mult).then_inc(s_gap2, 1)

            def variances(g):
                dve.wait_ge(s_gap2, g.index + 1)
                dve.wait_ge(s_within, g.index + 1)
                us = slice(g.first, g.first + g.count)
                nc.vector.scalar_tensor_tensor(out=spread[:, us], in0=gap[:, us], scalar=D / 4.0, in1=within[:, us],
                                               op0=ALU.mult, op1=ALU.add).then_inc(s_var, 1)

            def invert(g):
                dve.wait_ge(s_std, g.index + 1)
                us = slice(g.first, g.first + g.count)
                nc.vector.reciprocal(guess[:, us], std[:, us]).then_inc(s_n[0], 1)

            def other_root(g):
                dve.wait_ge(s_n[0], g.index + 1)
                us = slice(g.first, g.first + g.count)
                nc.vector.scalar_tensor_tensor(out=square[:, us], in0=spread[:, us], scalar=D * EPS,
                                               in1=guess[:, us], op0=ALU.add, op1=ALU.mult).then_inc(s_n[1], 1)

            def add_roots(g):
                dve.wait_ge(s_n[1], g.index + 1)
                us = slice(g.first, g.first + g.count)
                nc.vector.tensor_tensor(square[:, us], square[:, us], std[:, us], ALU.add).then_inc(s_n[2], 1)

            def invert_sum(g):
                dve.wait_ge(s_n[2], g.index + 1)
                us = slice(g.first, g.first + g.count)
                nc.vector.reciprocal(half[:, us], square[:, us]).then_inc(s_n[3], 1)

            def scale_and_shift(g):
                dve.wait_ge(s_n[3], g.index + 1)
                us = slice(g.first, g.first + g.count)
                nc.vector.tensor_scalar(rstd[:, g.batch.side, us], half[:, us], 2 * D ** 0.5, None, ALU.mult)
                nc.vector.scalar_tensor_tensor(out=shift[:, g.batch.side, us], in0=mean2[:, us], scalar=-D ** 0.5,
                                               in1=half[:, us], op0=ALU.mult, op1=ALU.mult).then_inc(s_rstd, 1)

            def normalise(g, units):
                dve.wait_ge(s_rstd, g.index + 1)
                for v in units:
                    last = nc.vector.tensor_scalar(rows[:, g.batch.side, v, :], rows[:, g.batch.side, v, :],
                                                   rstd[:, g.batch.side, v:v + 1], shift[:, g.batch.side, v:v + 1],
                                                   ALU.mult, ALU.add)
                last.then_inc(s_done, 1)

            def finish(oldest, older, old, a, b, c):
                mask_unit(b, GU)
                invert(older)
                other_root(older)
                mask_unit(b, GU + 1)
                add_roots(older)
                invert_sum(older)
                mask_unit(c, GU + 2)
                scale_and_shift(older)
                sum_rows(old)
                mask_unit(c, GU + 3)
                statistics(old)
                compare(a.batch)
                combine(old)
                variances(old)
                invert(old)
                other_root(old)
                sum_rows(a)
                add_roots(old)
                statistics(a)
                invert_sum(old)
                combine(a)
                scale_and_shift(old)
                variances(a)
                both = joined(b, c)
                invert(a)
                other_root(a)
                sum_rows(both)
                add_roots(a)
                statistics(both)
                invert_sum(a)
                combine(both)
                scale_and_shift(a)
                variances(both)
                dve.wait_ge(s_cmp, B)
                nc.vector.tensor_tensor(excess[:, :], excess[:, :], unsuited[:, :], ALU.max).then_inc(s_both, 1)
                dve.wait_ge(s_both, 1)
                nc.vector.tensor_reduce(worst[:, :], excess[:, :], AX.X, ALU.max).then_inc(s_worst, 1)
                invert(both)
                dve.wait_ge(s_worst, 1)
                nc.vector.tensor_scalar(found[:, :], worst[:, :], 0.0, None, ALU.is_gt).then_inc(s_found, 1)
                other_root(both)
                add_roots(both)
                invert_sum(both)
                scale_and_shift(both)
                normalise(both, c.units)
                dve.wait_ge(s_count, 1)
                nc.vector.tensor_copy(again[:, :], ids_t[0][0:1, 0, 0:2].bitcast(FP32)).then_inc(s_again, 1)

            def step(g, coming, before, earlier, nxt):
                after = coming[0]
                due = list(after.units) if after else []
                ready = nxt if g.place == 0 else None

                def do(part, what):
                    if what:
                        part(what)

                def mask_next():
                    if due:
                        mask_unit(after, due.pop(0))

                do(scale_maxima, ready)
                mask_next()
                do(invert, earlier)
                do(scale_largest, ready)
                do(other_root, earlier)
                do(scale_power, ready)
                do(add_roots, earlier)
                do(scale_down, ready)
                mask_next()
                do(scale_up, ready)
                do(invert_sum, earlier)
                do(scale_and_shift, earlier)
                mask_next()
                do(sum_rows, before)
                mask_next()
                do(scale_unsuited, ready)
                do(statistics, before)
                do(combine, before)
                do(variances, before)
                if after is not None and after.batch is g.batch and after.place == len(g.batch.groups) - 1:
                    compare(g.batch)
            s_rm, s_mx, s_pw, s_dn = (sem(n) for n in ("row_max_ready", "largest_ready", "power_ready", "down_ready"))
            s_far, s_far2, s_uns, s_both = (sem(n) for n in ("far_ready", "far_nonzero", "unsuited_ready", "both_ready"))
            s_st = sem("stats_ready")
            s_gap, s_gap2, s_within = (sem(n) for n in ("gap_ready", "gap_squared", "within_ready"))
            s_cmp = sem("batches_compared")
            s_worst = sem("worst_ready")
            s_n = [sem(f"root{n}") for n in range(4)]
            nc.vector.memset(eps[:, :], D * EPS)
            nc.vector.memset(ones[:, :], 1.0)
            nc.vector.memset(excess[:, :], 0.0)
            nc.vector.memset(unsuited[:, :], 0.0).then_inc(s_const, 1)
            dve.wait_ge(s_const, 1)
            dve.sem_inc(s_sum, 1)
            start = Batch(0, 0, 0, STEADY, NG)
            for part in (scale_maxima, scale_largest, scale_power, scale_down, scale_up, scale_unsuited):
                part(start)
            mask_unit(start.groups[0], 0)
            for u in start.groups[0].units[1:]:
                mask_unit(start.groups[0], u)
            walk(dve, step, finish)

        first_pass.close()

        g_w = sem("g_weights_loaded")
        g_x = sem("g_x_loaded")
        g_adj = [sem(f"g_adj_loaded{n}") for n in range(PAIRS)]
        g_out, g_batch = sem("g_rows_stored"), sem("g_batches_stored")
        g_hi, g_rest, g_mid, g_lo, g_xb = (sem(f"g_{n}_ready") for n in ("hi", "rest", "mid", "lo", "xb"))
        g_cast, g_tr, g_mask = sem("g_units_cast"), sem("g_units_transposed"), sem("g_units_masked")
        g_prod, g_h, g_y = sem("g_products_done"), sem("g_h_copied"), sem("g_projected")
        g_sum, g_stats, g_gap, g_var = sem("g_summed"), sem("g_stats"), sem("g_gap"), sem("g_var")
        g_std, g_norm = sem("g_std"), sem("g_normalised")
        g_root = [sem(f"g_root{n}") for n in range(5)]
        g_gap2 = sem("g_gap_squared")

        parts = [x_hi[:, 0].bitcast(BF16), x_hi[:, 1].bitcast(BF16), x_lo[:, 0].bitcast(BF16)]
        rest = xb[:, 1]

        def halves(t, n):
            return t[..., n * GU * P:(n + 1) * GU * P]

        def second_pass():
            with nc.Block() as block:
                @block.sync
                def _(sp):
                    sp.dma_start(w_sb[:, 1:R, :], weight[1:R].rearrange("r d o -> d r o")).then_inc(g_w, 16)
                    with sp.Fori(0, B) as b:
                        sp.dma_start(x_sb[:, 0], x_d[b]).then_inc(g_x, 16)
                        for k in range(PAIRS):
                            sp.dma_start(adj_sb[:, 0, 2 * k:2 * k + 2, :],
                                         adj_d[b, :, 2 * k:2 * k + 2, :]).then_inc(g_adj[k], 16)
                        for g in range(NG):
                            sp.wait_ge(g_norm, NG * b + g + 1)
                            sp.dma_start(out_d[b, :, g * GU:(g + 1) * GU, :],
                                         rows[:, 0, g * GU:(g + 1) * GU, :]).then_inc(g_out, 16)
                        sp.wait_ge(g_out, 16 * NG * (b + 1))
                        sp.sem_inc(g_batch, 1)

                @block.gpsimd
                def _(pool):
                    with pool.Fori(0, B) as b:
                        pool.wait_ge(g_x, 16 * (b + 1))
                        nc.gpsimd.tensor_tensor(xb[:, 0], x_sb[:, 0],
                                                bias_sb[:, :].unsqueeze(1).to_broadcast([P, J, D]),
                                                ALU.add).then_inc(g_xb, 1)

                @block.scalar
                def _(act):
                    with act.Fori(0, B) as b:
                        for u in range(J):
                            act.wait_ge(g_adj[u // 2], 16 * (b + 1))
                            nc.scalar.activation(ids[:, u], adj_sb[:, 0, u, :].rearrange("p (q j) -> p j q", j=J),
                                                 ACT.Relu).then_inc(g_cast, 1)
                        act.wait_ge(g_x, 16 * (b + 1))
                        nc.scalar.activation(parts[0], x_sb[:, 0], ACT.Copy).then_inc(g_hi, 1)
                        for g in range(NG):
                            for r in range(R):
                                done = R * (NG * b + g) + r
                                act.wait_ge(g_prod, done + 1)
                                nc.scalar.activation(h_all[:, r, :], h_ps[r % 2][:, :], ACT.Copy).then_inc(g_h, 1)
                            act.wait_ge(g_var, NG * b + g + 1)
                            us = slice(g * GU, (g + 1) * GU)
                            nc.scalar.activation(std[:, us], spread[:, us], ACT.Sqrt,
                                                 bias=eps[:, 0:1]).then_inc(g_std, 1)

                @block.tensor
                def _(pe):
                    pe.wait_ge(g_w, 16)
                    with pe.Fori(0, B) as b:
                        for g in range(NG):
                            for n in range(GU):
                                pe.wait_ge(g_cast, J * b + GU * g + n + 1)
                                if g:
                                    pe.wait_ge(g_mask, R * GU * (NG * b + g))
                                for j in range(J):
                                    last = nc.tensor.transpose(ids_t[n][:, j, :], ids[:, g * GU + n, j, :], ident[:, :])
                                last.then_inc(g_tr, 1)
                            pe.wait_ge(g_hi, b + 1)
                            pe.wait_ge(g_lo, b + 1)
                            for r in range(R):
                                done = R * (NG * b + g) + r
                                pe.wait_ge(g_mask, GU * (done + 1))
                                if r >= 2:
                                    pe.wait_ge(g_h, done - 1)
                                for j in range(J):
                                    for n, part in enumerate(parts):
                                        last = nc.tensor.matmul(
                                            h_ps[r % 2][:, :], part[:, j, :], halves(mask_t[:, j, :], r % 2),
                                            start=(j == 0 and n == 0), stop=(j == J - 1 and n == len(parts) - 1))
                                last.then_inc(g_prod, 1)
                            pe.wait_ge(g_h, R * (NG * b + g + 1))
                            for n in range(GU):
                                for r in range(R):
                                    last = nc.tensor.matmul(y_ps[0][:, n, :], h_all[:, r, n * P:(n + 1) * P],
                                                            w_sb[:, r, :], start=(r == 0), stop=(r == R - 1))
                            last.then_inc(g_y, 1)

                @block.vector
                def _(dve):
                    with dve.Fori(0, B) as b:
                        dve.wait_ge(g_hi, b + 1)
                        nc.vector.tensor_tensor(rest, x_sb[:, 0], parts[0], ALU.subtract).then_inc(g_rest, 1)
                        dve.wait_ge(g_rest, b + 1)
                        nc.vector.tensor_copy(parts[1], rest).then_inc(g_mid, 1)
                        dve.wait_ge(g_mid, b + 1)
                        nc.vector.tensor_tensor(parts[2], rest, parts[1], ALU.subtract).then_inc(g_lo, 1)
                        for g in range(NG):
                            us = slice(g * GU, (g + 1) * GU)
                            for r in range(R):
                                if r >= 2:
                                    dve.wait_ge(g_prod, R * (NG * b + g) + r - 1)
                                for n in range(GU):
                                    dve.wait_ge(g_tr, J * b + GU * g + n + 1)
                                    at = (r % 2 * GU + n) * P
                                    nc.vector.tensor_scalar(mask_t[:, :, at:at + P], ids_t[n][:, :, :], float(r + 1),
                                                            None, ALU.is_equal).then_inc(g_mask, 1)
                            dve.wait_ge(g_xb, b + 1)
                            dve.wait_ge(g_y, NG * b + g + 1)
                            nc.vector.tensor_tensor(rows[:, 0, us, :], y_ps[0][:, :, :], xb[:, 0, us, :], ALU.add).then_inc(g_sum, 1)
                            dve.wait_ge(g_sum, NG * b + g + 1)
                            for u in range(g * GU, (g + 1) * GU):
                                last = nc.vector.bn_stats(stats[:, u, :], rows[:, 0, u, :])
                            last.then_inc(g_stats, 1)
                            dve.wait_ge(g_stats, NG * b + g + 1)
                            even, odd = stats[:, us, 0:3], stats[:, us, 3:6]
                            nc.vector.tensor_tensor(gap[:, us], even[:, :, 1], odd[:, :, 1], ALU.subtract)
                            nc.vector.tensor_tensor(mean2[:, us], even[:, :, 1], odd[:, :, 1], ALU.add)
                            nc.vector.tensor_tensor(within[:, us], even[:, :, 2], odd[:, :, 2], ALU.add).then_inc(g_gap, 1)
                            dve.wait_ge(g_gap, NG * b + g + 1)
                            nc.vector.tensor_tensor(gap[:, us], gap[:, us], gap[:, us], ALU.mult).then_inc(g_gap2, 1)
                            dve.wait_ge(g_gap2, NG * b + g + 1)
                            nc.vector.scalar_tensor_tensor(out=spread[:, us], in0=gap[:, us], scalar=D / 4.0,
                                                           in1=within[:, us], op0=ALU.mult, op1=ALU.add).then_inc(g_var, 1)
                            dve.wait_ge(g_std, NG * b + g + 1)
                            nc.vector.reciprocal(guess[:, us], std[:, us]).then_inc(g_root[0], 1)
                            dve.wait_ge(g_root[0], NG * b + g + 1)
                            nc.vector.scalar_tensor_tensor(out=square[:, us], in0=spread[:, us], scalar=D * EPS,
                                                           in1=guess[:, us], op0=ALU.add, op1=ALU.mult).then_inc(g_root[1], 1)
                            dve.wait_ge(g_root[1], NG * b + g + 1)
                            nc.vector.tensor_tensor(square[:, us], square[:, us], std[:, us], ALU.add).then_inc(g_root[2], 1)
                            dve.wait_ge(g_root[2], NG * b + g + 1)
                            nc.vector.reciprocal(half[:, us], square[:, us]).then_inc(g_root[3], 1)
                            dve.wait_ge(g_root[3], NG * b + g + 1)
                            nc.vector.tensor_scalar(rstd[:, 0, us], half[:, us], 2 * D ** 0.5, None, ALU.mult)
                            nc.vector.scalar_tensor_tensor(out=shift[:, 0, us], in0=mean2[:, us], scalar=-D ** 0.5,
                                                           in1=half[:, us], op0=ALU.mult, op1=ALU.mult).then_inc(g_root[4], 1)
                            dve.wait_ge(g_root[4], NG * b + g + 1)
                            for u in range(g * GU, (g + 1) * GU):
                                last = nc.vector.tensor_scalar(rows[:, 0, u, :], rows[:, 0, u, :], rstd[:, 0, u:u + 1],
                                                               shift[:, 0, u:u + 1], ALU.mult, ALU.add)
                            last.then_inc(g_norm, 1)

        high = nc.values_load(again[0:1, 0:1], min_val=0, max_val=P)
        with nc.If(high > 0):
            second_pass()


def kernel(x, adj, L0_gnn_adj, L0_gnn_weight, L0_gnn_bias):
    import numpy as np
    import concourse.bacc as bacc
    from concourse.bass_utils import run_bass_kernel_spmd

    nc = bacc.Bacc("TRN2", target_bir_lowering=False, num_devices=1)
    arrays = {"x": np.ascontiguousarray(x), "adj": np.ascontiguousarray(adj),
              "weight": np.ascontiguousarray(L0_gnn_weight), "bias": np.ascontiguousarray(L0_gnn_bias)}
    args = [nc.dram_tensor(name, a.shape, mybir.dt.from_np(a.dtype), kind="ExternalInput").ap()
            for name, a in arrays.items()]
    out = nc.dram_tensor("out", arrays["x"].shape, FP32, kind="ExternalOutput").ap()
    adj_resnorm_kernel(nc, *args, out)
    return run_bass_kernel_spmd(nc, [arrays], core_ids=[0]).results[0]["out"]
```
